# Optimizing a Trainium2 kernel written in Bass

```python
import numpy as np
import jax
import jax.numpy as jnp

def _softmax(x, axis=-1):
    return jax.nn.softmax(x, axis=axis)

def _gelu(x):
    return jax.nn.gelu(x, approximate=True)

def _silu(x):
    return jax.nn.silu(x)

def _sigmoid(x):
    return jax.nn.sigmoid(x)

def _layernorm(x, axis=-1, eps=1e-05):
    m = jnp.mean(x, axis=axis, keepdims=True)
    v = jnp.var(x, axis=axis, keepdims=True)
    return (x - m) / jnp.sqrt(v + eps)

def _scatter_add(tgt, idx, src, axis=0):
    return tgt.at[idx].add(src)

def _segment_sum(src, seg, n):
    return jax.ops.segment_sum(src, seg, n)
kernel_name = 'mk_xattn_ffn_d1_seqx_r2_4be80b'

def setup_inputs(seed: int=0):
    np.random.seed(seed)
    _w = jnp.asarray

    def _rec_inputs():
        import jax
        import jax.numpy as jnp
        _rk = jax.random.key(seed)
        x = -0.0002928 + 1 * jax.random.normal(jax.random.fold_in(_rk, 1), (2, 2048, 512), jnp.float32)
        _lenS = 2048 - jax.random.randint(jax.random.fold_in(_rk, 7), (2,), 0, max(1, 2048 // 4) + 1, jnp.int32)
        _lenS2 = 77 - jax.random.randint(jax.random.fold_in(_rk, 8), (2,), 0, max(1, 77 // 4) + 1, jnp.int32)
        _ctx_1024P = jax.random.normal(jax.random.fold_in(_rk, 11), (2, 16, 512), jnp.float32)
        _ctx_1024c = jax.random.dirichlet(jax.random.fold_in(_rk, 511), 0.3 * jnp.ones((16,), jnp.float32), (2, 77))
        _ctx_1024t = jnp.einsum('bsk,bkd->bsd', _ctx_1024c, _ctx_1024P)
        _ctx_1024t = _ctx_1024t * jax.lax.rsqrt(jnp.mean(jnp.square(_ctx_1024t)) + 1e-12) * 0.953939
        ctx_1024 = -1.39393e-06 + 0.999914 * (_ctx_1024t + 0.3 * jax.random.normal(jax.random.fold_in(_rk, 611), (2, 77, 512), jnp.float32))
        return (x, ctx_1024)
    x, ctx_1024 = _rec_inputs()

    def _L0_xattn_setup():
        import jax, jax.numpy as jnp
        import numpy as np
        D_MODEL = 512
        N_HEADS = 16
        D_K = D_MODEL // N_HEADS
        key = jax.random.key(seed)
        ks = jax.random.split(key, 11)
        B, L, S = (2, 1024, 1024)
        scale = 1.0 / np.sqrt(D_MODEL)
        return {'x_q': jax.random.normal(ks[0], (B, L, D_MODEL), jnp.float32), 'x_k': jax.random.normal(ks[1], (B, S, D_MODEL), jnp.float32), 'x_v': jax.random.normal(ks[2], (B, S, D_MODEL), jnp.float32), 'W_Q': jax.random.normal(ks[3], (D_MODEL, D_MODEL), jnp.float32) * scale, 'b_Q': jax.random.normal(ks[4], (D_MODEL,), jnp.float32) * 0.01, 'W_K': jax.random.normal(ks[5], (D_MODEL, D_MODEL), jnp.float32) * scale, 'b_K': jax.random.normal(ks[6], (D_MODEL,), jnp.float32) * 0.01, 'W_V': jax.random.normal(ks[7], (D_MODEL, D_MODEL), jnp.float32) * scale, 'b_V': jax.random.normal(ks[8], (D_MODEL,), jnp.float32) * 0.01, 'W_O': jax.random.normal(ks[9], (D_MODEL, D_MODEL), jnp.float32) * scale, 'b_O': jax.random.normal(ks[10], (D_MODEL,), jnp.float32) * 0.01}
    _L0_xattn_all = _L0_xattn_setup()
    _L0_xattn_in = {k: v for k, v in _L0_xattn_all.items() if k in ('W_Q', 'b_Q', 'W_K', 'b_K', 'W_V', 'b_V', 'W_O', 'b_O')}
    del _L0_xattn_all

    def _L0_ffn_setup():
        import jax, jax.numpy as jnp
        import numpy as np
        D_MODEL = 512
        DEPTH = 8
        M = 2 ** DEPTH
        N_INTERNAL = M - 1
        B, T = (8, 2048)

        def _leaf_probs(gate):
            BT = gate.shape[0]
            lp = jnp.ones((BT, M), dtype=gate.dtype)
            for level in range(DEPTH):
                n = 2 ** level
                half = M // (2 * n)
                g = gate[:, n - 1:2 * n - 1]
                f = jnp.stack([1.0 - g, g], axis=-1)
                f = jnp.broadcast_to(f[..., None], (BT, n, 2, half))
                lp = lp * f.reshape(BT, M)
            return lp
        key = jax.random.key(seed)
        ks = jax.random.split(key, 7)
        x = jax.random.normal(ks[0], (B, T, D_MODEL), dtype=jnp.float32)
        Wq = jax.random.normal(ks[1], (D_MODEL, D_MODEL), dtype=jnp.float32) * 0.02
        routers = jax.random.normal(ks[2], (N_INTERNAL, D_MODEL), dtype=jnp.float32) * 0.02
        leaf_keys = jax.random.normal(ks[3], (M, D_MODEL), dtype=jnp.float32) * 0.02
        leaf_values = jax.random.normal(ks[4], (M, D_MODEL), dtype=jnp.float32) * 0.02
        Wout_w = jax.random.normal(ks[5], (D_MODEL, D_MODEL), dtype=jnp.float32) * 0.02
        Wout_b = jax.random.normal(ks[6], (D_MODEL,), dtype=jnp.float32) * 0.02
        return {'x': x, 'Wq': Wq, 'routers': routers, 'leaf_keys': leaf_keys, 'leaf_values': leaf_values, 'Wout_w': Wout_w, 'Wout_b': Wout_b}
    _L0_ffn_all = _L0_ffn_setup()
    _L0_ffn_in = {k: v for k, v in _L0_ffn_all.items() if k in ('Wq', 'routers', 'leaf_keys', 'leaf_values', 'Wout_w', 'Wout_b')}
    del _L0_ffn_all
    return {'x': x, 'ctx_1024': ctx_1024, 'L0_xattn_W_Q': _L0_xattn_in['W_Q'], 'L0_xattn_b_Q': _L0_xattn_in['b_Q'], 'L0_xattn_W_K': _L0_xattn_in['W_K'], 'L0_xattn_b_K': _L0_xattn_in['b_K'], 'L0_xattn_W_V': _L0_xattn_in['W_V'], 'L0_xattn_b_V': _L0_xattn_in['b_V'], 'L0_xattn_W_O': _L0_xattn_in['W_O'], 'L0_xattn_b_O': _L0_xattn_in['b_O'], 'L0_ffn_Wq': _L0_ffn_in['Wq'], 'L0_ffn_routers': _L0_ffn_in['routers'], 'L0_ffn_leaf_keys': _L0_ffn_in['leaf_keys'], 'L0_ffn_leaf_values': _L0_ffn_in['leaf_values'], 'L0_ffn_Wout_w': _L0_ffn_in['Wout_w'], 'L0_ffn_Wout_b': _L0_ffn_in['Wout_b']}

def reference(x, ctx_1024, L0_xattn_W_Q, L0_xattn_b_Q, L0_xattn_W_K, L0_xattn_b_K, L0_xattn_W_V, L0_xattn_b_V, L0_xattn_W_O, L0_xattn_b_O, L0_ffn_Wq, L0_ffn_routers, L0_ffn_leaf_keys, L0_ffn_leaf_values, L0_ffn_Wout_w, L0_ffn_Wout_b):
    import jax
    import jax.numpy as jnp

    def _L0_xattn_ref(x_q, x_k, x_v, W_Q, b_Q, W_K, b_K, W_V, b_V, W_O, b_O):
        import jax, jax.numpy as jnp
        import numpy as np
        D_MODEL = 512
        N_HEADS = 16
        D_K = D_MODEL // N_HEADS
        B, L, _ = x_q.shape
        S = x_k.shape[1]
        H, dk = (N_HEADS, D_K)
        Q = (x_q @ W_Q + b_Q).reshape(B, L, H, dk).transpose(0, 2, 1, 3)
        K = (x_k @ W_K + b_K).reshape(B, S, H, dk).transpose(0, 2, 1, 3)
        V = (x_v @ W_V + b_V).reshape(B, S, H, dk).transpose(0, 2, 1, 3)
        scores = jnp.einsum('bhld,bhsd->bhls', Q, K) / jnp.sqrt(jnp.float32(dk))
        attn = jax.nn.softmax(scores, axis=-1)
        ctx = jnp.einsum('bhls,bhsd->bhld', attn, V)
        ctx = ctx.transpose(0, 2, 1, 3).reshape(B, L, H * dk)
        out = ctx @ W_O + b_O
        return out

    def _L0_ffn_ref(x, Wq, routers, leaf_keys, leaf_values, Wout_w, Wout_b):
        import jax, jax.numpy as jnp
        import numpy as np
        D_MODEL = 512
        DEPTH = 8
        M = 2 ** DEPTH
        N_INTERNAL = M - 1
        B, T = (8, 2048)

        def _leaf_probs(gate):
            BT = gate.shape[0]
            lp = jnp.ones((BT, M), dtype=gate.dtype)
            for level in range(DEPTH):
                n = 2 ** level
                half = M // (2 * n)
                g = gate[:, n - 1:2 * n - 1]
                f = jnp.stack([1.0 - g, g], axis=-1)
                f = jnp.broadcast_to(f[..., None], (BT, n, 2, half))
                lp = lp * f.reshape(BT, M)
            return lp
        Bv, Tv, d = x.shape
        q = jnp.einsum('btd,ed->bte', x, Wq)
        q_flat = q.reshape(Bv * Tv, d)
        gate = jax.nn.sigmoid(q_flat @ routers.T)
        leaf_prob = _leaf_probs(gate)
        ret = (leaf_prob @ leaf_values).reshape(Bv, Tv, d)
        return jnp.einsum('btd,ed->bte', ret, Wout_w) + Wout_b
    x = x + _L0_xattn_ref(_layernorm(x, axis=-1), ctx_1024, ctx_1024, L0_xattn_W_Q, L0_xattn_b_Q, L0_xattn_W_K, L0_xattn_b_K, L0_xattn_W_V, L0_xattn_b_V, L0_xattn_W_O, L0_xattn_b_O)
    x = x + _L0_ffn_ref(_layernorm(x, axis=-1), L0_ffn_Wq, L0_ffn_routers, L0_ffn_leaf_keys, L0_ffn_leaf_values, L0_ffn_Wout_w, L0_ffn_Wout_b)
    return x

_drawn_inputs = setup_inputs


def setup_inputs(seed=0):
    import zlib

    import numpy as np

    out = dict(_drawn_inputs(seed))
    spreads = {}
    factors = {'L0_xattn_b_Q': 8.0,
     'L0_xattn_b_K': 8.0,
     'L0_xattn_b_V': 6.784,
     'L0_xattn_b_O': 6.252,
     'L0_ffn_Wq': 8.0,
     'L0_ffn_routers': 8.0,
     'L0_ffn_leaf_values': 8.0,
     'L0_ffn_Wout_w': 8.0,
     'L0_ffn_Wout_b': 3.165}
    for name, (base, spread) in spreads.items():
        noise = np.random.default_rng([zlib.crc32(name.encode()), seed]).standard_normal(out[name].shape)
        drawn = base * np.exp(spread * noise) if base else spread * noise
        out[name] = jnp.asarray(drawn.astype(out[name].dtype))
    for name, factor in factors.items():
        out[name] = (out[name] * factor).astype(out[name].dtype)
    return out
```

```python
from contextlib import ExitStack

import numpy as np

import concourse.bass as bass
from concourse import mybir

F32 = mybir.dt.float32
F16 = mybir.dt.float16
ALU = mybir.AluOpType
ACT = mybir.ActivationFunctionType
AX_X = mybir.AxisListType.X
RMAX = bass.bass_isa.ReduceOp.max

P = 128
B, L, S, D = 2, 2048, 77, 512
H, DK = 16, 32
KC = D // P
NT = B * L // P
TPB = NT // B
XQ = 4
NQ = NT // XQ
HG = P // DK
NG = H // HG
GS = HG * S
RC = 3
CR = -(-GS // RC)
VW = DK + 1
DEPTH = 8
M = 2 ** DEPTH
NI = M - 1
LC = M // P
NP = NT // 2
TARGET = 64.0
ROOT = 2.0 ** 15
EPS = 1e-5
PASSES = [(0, 0), (1, 0), (0, 1)]


def build(nc, x, ctxT, W_Q, b_Q, W_K, b_K, W_V, b_V, W_O, b_O, Wq, routersT, leafvT, WoutT, Wout_b,
          eye, eye16, ones_cols, out):
    ctx = ExitStack()
    with ctx:
        def sb(name, shape, dt=F32):
            return ctx.enter_context(nc.sbuf_tensor(name, shape, dt))

        def sem(name):
            return ctx.enter_context(nc.semaphore(name))

        xs = sb("xs", [P, NT * D])
        ident = sb("ident", [P, P])
        ident16 = sb("ident16", [P, P], F16)
        wq_f = sb("wq_f", [P, KC, D])
        wk_f = sb("wk_f", [P, KC, D])
        wv_f = sb("wv_f", [P, KC, D])
        wo_f = sb("wo_f", [P, KC, D])
        fq_f = sb("fq_f", [P, KC, D])
        wout_f = sb("wout_f", [P, KC, D])
        rt_f = sb("rt_f", [P, KC, NI])
        lf_f = sb("lf_f", [P, KC, M])
        cT = sb("cT", [P, KC, B * S])
        bq_c = sb("bq_c", [P, KC])
        bk_c = sb("bk_c", [P, KC])
        bv_room = sb("bv_room", [P, D])
        bv_r = bv_room[0:S]
        bo_r = sb("bo_r", [P, D])
        bout_r = sb("bout_r", [P, D])
        wq_s = sb("wq_s", [P, 2, KC, D], F16)
        wo_s = sb("wo_s", [P, 2, KC, D], F16)
        g_s = sb("g_s", [P, 2, KC, NI + 1], F16)
        lv_s = sb("lv_s", [P, 2, LC, D], F16)
        kf = sb("kf", [P, KC, B * S])
        kd = sb("kd", [P, B, 2, NG, GS], F16)
        vf = sb("vf", [S, B, D])
        v_room = sb("v_room", [P, B, 2, D], F16)
        vh = v_room[0:S]
        vd = sb("vd", [P, RC, B, 2, NG, 2, VW], F16)
        oc = sb("oc", [P, RC, 2], F16)
        am = sb("am", [P, 8])
        ar = sb("ar", [P, 8])
        inv = sb("inv", [P, 8])
        sc = sb("sc", [P, 8])
        dq = sb("dq", [P, 8])
        st6 = sb("st6", [P, 2, 6])
        mv = sb("mv", [P, 2, 2])
        veps = sb("veps", [P, 2])
        mhalf = sb("mhalf", [P, 2])
        eps = sb("eps", [P, 2])
        rstd = sb("rstd", [P, 2])
        xn = sb("xn", [P, 2, D])
        xnh = sb("xnh", [P, 2, 2, D], F16)
        xT = sb("xT", [P, 2, 2 * KC * P], F16)
        qT = sb("qT", [P, 2, 2, KC, P], F16)
        mx = sb("mx", [P, 2, HG])
        df = sb("df", [P, 2, GS])
        pr = sb("pr", [P, 2, RC * CR])
        pT = sb("pT", [P, 2, 2, RC * P], F16)
        rden = sb("rden", [P, 2, H // 2])
        cx = sb("cx", [P, D])
        cxh = sb("cxh", [P, 2, D], F16)
        cxT = v_room[:, 0].rearrange("p a n -> p (a n)")
        lT = v_room[:, 1].rearrange("p a n -> p (a n)")
        lph = bv_room[:].bitcast(F16).rearrange("p (t a m) -> p t a m", t=2, a=2)
        ob = wk_f[:].rearrange("p (a t) n -> p a t n", a=2)
        wv_room = wv_f[:].rearrange("p c n -> p (c n)")
        lp = [wv_room[:, n * 2 * M:(n + 1) * 2 * M].rearrange("p (t m) -> p t m", t=2) for n in range(2)]
        fr = wv_room[:, 4 * M:4 * M + 4 * NI].rearrange("p (t s n) -> p t s n", t=2, s=2)
        th = kf[:].rearrange("p c s -> p (c s)")[:, 0:2 * NI].rearrange("p (t n) -> p t n", t=2)
        bank = ctx.enter_context(nc.psum_tensor("bank", [P, 8, 512], F32))

        def tile_of_x(i):
            return xs[:, bass.ds(i * D, D)]

        small_in, cT_in, wk_in, wq_in, wv_in, wo_in = (sem(n) for n in (
            "small_in", "cT_in", "wk_in", "wq_in", "wv_in", "wo_in"))
        fq_in, rt_in, wout_in, lf_in, late_in = (sem(n) for n in ("fq_in", "rt_in", "wout_in", "lf_in", "late_in"))
        x_in = [sem(f"x_in{q}") for q in range(NQ)]
        x_here = sem("x_here")
        consts_set = sem("consts_set")
        k_mm, v_mm, g_mm, lv_mm = (sem(n) for n in ("k_mm", "v_mm", "g_mm", "lv_mm"))
        kf_done, vf_done = sem("kf_done"), sem("vf_done")
        absmax_done, allmax_done, scale_step = sem("absmax_done"), sem("allmax_done"), sem("scale_step")
        scaled = [sem(f"scaled{n}") for n in range(6)]
        hi_set = [sem(f"hi_set{n}") for n in range(6)]
        lo_set = [sem(f"lo_set{n}") for n in range(6)]
        vd_zero, vd_ones, vd_in = sem("vd_zero"), sem("vd_ones"), sem("vd_in")
        kd_zero = sem("kd_zero")
        stats_done, aggr_done, veps_done, rstd_done, xn_done, xnh_done, xnl_done, xb_done = (sem(n) for n in (
            "stats_done", "aggr_done", "veps_done", "rstd_done", "xn_done", "xnh_done", "xnl_done", "xb_done"))
        xT_mm, xT_ready, q_mm, qh_done, ql_done = (sem(n) for n in ("xT_mm", "xT_ready", "q_mm", "qh_done", "ql_done"))
        s_mm, max_done, sub_done, exp_done, pT_mm, pTh_done, pTl_done, pv_mm = (sem(n) for n in (
            "s_mm", "max_done", "sub_done", "exp_done", "pT_mm", "pTh_done", "pTl_done", "pv_mm"))
        rden_done, cx_done, cxh_done, cxl_done, cxT_mm, cxT_ready, wo_mm, x2_done = (sem(n) for n in (
            "rden_done", "cx_done", "cxh_done", "cxl_done", "cxT_mm", "cxT_ready", "wo_mm", "x2_done"))
        b_stats, b_aggr, b_veps, b_rstd, b_xn, b_xnh, b_xnl, b_xb = (sem(n) for n in (
            "b_stats", "b_aggr", "b_veps", "b_rstd", "b_xn", "b_xnh", "b_xnl", "b_xb"))
        b_xT_mm, b_xT_ready, lg_mm, th_done, fr_done, lvl_done, lph_done, lpl_done = (sem(n) for n in (
            "b_xT_mm", "b_xT_ready", "lg_mm", "th_done", "fr_done", "lvl_done", "lph_done", "lpl_done"))
        lT_mm, lT_ready, mix_mm, ob_done = (sem(n) for n in ("lT_mm", "lT_ready", "mix_mm", "ob_done"))
        stored = [sem("stored0"), sem("stored1")]

        def wait(eng, s, v):
            if not isinstance(v, int) or v > 0:
                eng.wait_ge(s, v)

        WQ_, K_, V_, WO_, G_, LV_ = range(6)
        DQ_EXP, DQ_OUT, DQ_TANH, DQ_MIX = range(4)

        x_v = x.rearrange("b (q p t) d -> (b q) p (t d)", p=P, t=XQ)
        out_v = out.rearrange("b (q p t) d -> (b q) p (t d)", p=P, t=XQ)

        def chunked(w):
            return w.rearrange("(c p) n -> p c n", p=P)

        def s_bank(n2):
            return bank[:, n2, 0:GS]

        def pT_bank(n2):
            return bank[0:CR, 2 + n2, 0:RC * P]

        def o_bank(half):
            return bank[:, 4 + half, 0:H // 2 * VW]

        tr_bank = bank[:, 6, :].bitcast(F16)
        qw_bank = bank[:, 7, :]

        def iterations_a(eng, body):
            for i in range(-2, 2):
                body(i, i % 2, 0, 0)
            with eng.Fori(1, TPB // 2) as j:
                for par in range(2):
                    body(2 * j + par, par, 0, 0)
            for par in range(2):
                body(TPB + par, par, 1, par)
            with eng.Fori(TPB // 2 + 1, NT // 2 - 1) as j:
                for par in range(2):
                    body(2 * j + par, par, 1, 1)
            for i in range(NT - 2, NT + 2):
                body(i, i % 2, 1, 1)

        def has(i, *offs):
            return not isinstance(i, int) or all(0 <= i + o < NT for o in offs)

        def iterations_b(eng, body):
            for j in range(-2, 2):
                body(j, j % 2, j // 2)
            with eng.Fori(1, NQ - 1) as q:
                for par in range(2):
                    body(2 * q + par, par, q)
            for j in range(NP - 2, NP + 1):
                body(j, j % 2, j // 2)

        def has_b(j, *offs):
            return not isinstance(j, int) or all(0 <= j + o < NP for o in offs)

        block = ctx.enter_context(nc.Block())

        @block.sync
        def _(sp):
            sp.dma_start(cT[:], chunked(ctxT)).then_inc(cT_in, 16)
            sp.dma_start(wk_f[:], chunked(W_K)).then_inc(wk_in, 16)
            sp.dma_start(xs[:, 0:XQ * D], x_v[0]).then_inc(x_in[0], 16)
            sp.dma_start(wv_f[:], chunked(W_V)).then_inc(wv_in, 16)
            for q in range(1, NQ):
                sp.dma_start(xs[:, q * XQ * D:(q + 1) * XQ * D], x_v[q]).then_inc(x_in[q], 16)
            for q in range(NQ):
                sp.wait_ge(x_in[q], 16)
                sp.sem_inc(x_here, 1)

            def body(j, par, q):
                if has_b(j, -1):
                    jq, jp = (q, 0) if par else (q - 1, 1)
                    wait(sp, ob_done, j)
                    sp.dma_start(out_v[jq, :, jp * 2 * D:(jp + 1) * 2 * D] if isinstance(jq, int)
                                 else out_v[bass.ds(jq, 1), :, jp * 2 * D:(jp + 1) * 2 * D].rearrange("o p d -> (o p) d"),
                                 ob[:, jp].rearrange("p t d -> p (t d)")).then_inc(stored[jp], 16)
            iterations_b(sp, body)
            for par in range(2):
                sp.wait_ge(stored[par], 16 * (NP // 2))

        @block.tensor
        def _(pe):
            pe.wait_ge(cT_in, 16)
            pe.wait_ge(wk_in, 16)
            for m in range(KC):
                for k in range(KC):
                    mm = nc.tensor.matmul(bank[:, m // 2, (m % 2) * B * S:(m % 2 + 1) * B * S],
                                          wk_f[:, k, m * P:(m + 1) * P], cT[:, k, :], start=(k == 0), stop=(k == KC - 1))
            mm.then_inc(k_mm, 1)
            pe.wait_ge(wv_in, 16)
            for b in range(B):
                for k in range(KC):
                    mm = nc.tensor.matmul(bank[0:S, 2 + b, :], cT[:, k, b * S:(b + 1) * S], wv_f[:, k, :],
                                          start=(k == 0), stop=(k == KC - 1))
            mm.then_inc(v_mm, 1)
            pe.wait_ge(consts_set, 32)
            pe.wait_ge(kf_done, 1)
            pe.wait_ge(vf_done, 1)

            def scores(i, g, par, b):
                n = 4 * i + g
                if g == 0:
                    wait(pe, qh_done, i + 1)
                    wait(pe, ql_done, i + 1)
                wait(pe, sub_done, n - 1)
                for a, w in PASSES:
                    mm = nc.tensor.matmul(s_bank(n2(g)), qT[:, par, a, g, :], kd[:, b, w, g, :],
                                          start=(a == w == 0), stop=(w == 1))
                mm.then_inc(s_mm, 1)

            def n2(g):
                return g % 2

            def probs_T(i, g):
                n = 4 * i + g
                wait(pe, exp_done, n + 1)
                wait(pe, pTh_done, n - 1)
                wait(pe, pTl_done, n - 1)
                for c in range(RC):
                    mm = nc.tensor.transpose(pT_bank(n2(g))[:, c * P:(c + 1) * P], pr[:, n2(g), c * CR:(c + 1) * CR], ident[:])
                mm.then_inc(pT_mm, 1)

            def pv(i, g, b):
                n = 4 * i + g
                wait(pe, pTh_done, n + 1)
                wait(pe, pTl_done, n + 1)
                if g % 2 == 0:
                    wait(pe, cx_done, 2 * i + g // 2 - 1)
                for c in range(RC):
                    at = ((g % 2) * HG + c) * VW
                    for a, w in PASSES:
                        mm = nc.tensor.matmul(
                            o_bank(g // 2)[:, at:at + 2 * VW], pT[0:CR, n2(g), a, c * P:(c + 1) * P],
                            vd[0:CR, c, b, w, g, :, :], start=(g % 2 == 0 and c == 0 and a == w == 0),
                            stop=(g % 2 == 1 and c == RC - 1 and w == 1), skip_group_check=True)
                mm.then_inc(pv_mm, 1)

            def x_T(i, par):
                wait(pe, xnh_done, i + 1)
                wait(pe, xnl_done, i + 1)
                wait(pe, cxT_ready, i - 2)
                for a in range(2):
                    for k in range(KC):
                        at = (a * KC + k) * P
                        mm = nc.tensor.transpose(tr_bank[:, at:at + P], xnh[:, 0, a, k * P:(k + 1) * P], ident16[:])
                mm.then_inc(xT_mm, 1)

            def q_chunks(i, ms):
                if ms[0] == 0:
                    wait(pe, xT_ready, i + 1)
                    wait(pe, x2_done, i - 2)
                for m in ms:
                    for n, (a, w) in enumerate(PASSES):
                        for k in range(KC):
                            at = (a * KC + k) * P
                            mm = nc.tensor.matmul(qw_bank[:, m * P:(m + 1) * P], wq_s[:, w, k, m * P:(m + 1) * P],
                                                  xT[:, 0, at:at + P], start=(n == k == 0), stop=(n == 2 and k == KC - 1))
                if ms[-1] == KC - 1:
                    mm.then_inc(q_mm, 1)

            def ctx_T(i):
                wait(pe, cxh_done, 2 * i + 2)
                wait(pe, cxl_done, 2 * i + 2)
                wait(pe, xT_ready, min(i + 3, NT) if isinstance(i, int) else i + 3)
                for a in range(2):
                    for k in range(KC):
                        at = (a * KC + k) * P
                        mm = nc.tensor.transpose(tr_bank[:, at:at + P], cxh[:, a, k * P:(k + 1) * P], ident16[:])
                mm.then_inc(cxT_mm, 1)

            def project(i, ks):
                if ks[0] == 0:
                    wait(pe, cxT_ready, i + 1)
                    wait(pe, qh_done, min(i + 3, NT) if isinstance(i, int) else i + 3)
                    wait(pe, ql_done, min(i + 3, NT) if isinstance(i, int) else i + 3)
                for k in ks:
                    for a, w in PASSES:
                        at = (a * KC + k) * P
                        mm = nc.tensor.matmul(qw_bank, cxT[:, at:at + P], wo_s[:, w, k, :],
                                              start=(k == a == w == 0), stop=(k == KC - 1 and w == 1))
                if ks[-1] == KC - 1:
                    mm.then_inc(wo_mm, 1)

            first = []

            def body(i, par, b, b_before):
                for g in range(NG):
                    if has(i, 0):
                        if isinstance(i, int) and i == 0 and g == 0:
                            pe.wait_ge(hi_set[K_], 1)
                            pe.wait_ge(lo_set[K_], 1)
                        scores(i, g, par, b)
                    if g == 0 and has(i, -1):
                        probs_T(i - 1, 3)
                    if g > 0 and has(i, 0):
                        probs_T(i, g - 1)
                    if g < 2 and has(i, -1):
                        pv(i - 1, g + 2, b_before)
                    if g >= 2 and has(i, 0):
                        if isinstance(i, int) and i == 0 and g == 2:
                            pe.wait_ge(vd_ones, 1)
                            pe.wait_ge(vd_in, 16 * 6)
                        pv(i, g - 2, b)
                    if g == 0:
                        if has(i, -2):
                            project(i - 2, [2, 3])
                        if has(i, 1):
                            x_T(i + 1, 1 - par)
                    if g == 1 and has(i, 1):
                        if not first:
                            first.append(1)
                            pe.wait_ge(hi_set[WQ_], 1)
                            pe.wait_ge(lo_set[WQ_], 1)
                        q_chunks(i + 1, [0, 1])
                    if g == 2:
                        if has(i, 1):
                            q_chunks(i + 1, [2, 3])
                        if has(i, -1):
                            ctx_T(i - 1)
                    if g == 3 and has(i, -1):
                        if isinstance(i, int) and i == 1:
                            pe.wait_ge(hi_set[WO_], 1)
                            pe.wait_ge(lo_set[WO_], 1)
                        project(i - 1, [0, 1])

            iterations_a(pe, body)

            pe.wait_ge(fq_in, 16)
            pe.wait_ge(rt_in, 16)
            pe.wait_ge(sub_done, 4 * NT)
            for m in range(KC):
                for k in range(KC):
                    mm = nc.tensor.matmul(bank[:, m // 2, (m % 2) * 256:(m % 2) * 256 + NI],
                                          fq_f[:, k, m * P:(m + 1) * P], rt_f[:, k, :], start=(k == 0), stop=(k == KC - 1))
            mm.then_inc(g_mm, 1)
            pe.wait_ge(wout_in, 16)
            pe.wait_ge(lf_in, 16)
            pe.wait_ge(pTh_done, 4 * NT)
            pe.wait_ge(pTl_done, 4 * NT)
            for m in range(LC):
                for k in range(KC):
                    mm = nc.tensor.matmul(bank[:, 2 + m, :], lf_f[:, k, m * P:(m + 1) * P], wout_f[:, k, :],
                                          start=(k == 0), stop=(k == KC - 1))
            mm.then_inc(lv_mm, 1)

            def body_b(j, par, q):
                if has_b(j, 0):
                    if isinstance(j, int) and j == 0:
                        pe.wait_ge(hi_set[G_], 1)
                        pe.wait_ge(lo_set[G_], 1)
                        pe.wait_ge(x2_done, NT)
                    wait(pe, b_xT_ready, j + 1)
                    wait(pe, th_done, j - 1)
                    for t in range(2):
                        for n, (a, w) in enumerate(PASSES):
                            for k in range(KC):
                                at = (a * KC + k) * P
                                mm = nc.tensor.matmul(bank[:, 6 + par, t * 256:t * 256 + NI], xT[:, t, at:at + P],
                                                      g_s[:, w, k, 0:NI], start=(n == k == 0), stop=(n == 2 and k == KC - 1))
                    mm.then_inc(lg_mm, 1)
                if has_b(j, -1):
                    if isinstance(j, int) and j == 1:
                        pe.wait_ge(scaled[G_], 1)
                    wait(pe, lph_done, j)
                    wait(pe, lpl_done, j)
                    wait(pe, lT_ready, j - 1)
                    for t in range(2):
                        for a in range(2):
                            for c in range(LC):
                                at = ((t * 2 + a) * LC + c) * P
                                mm = nc.tensor.transpose(bank[:, 0, :].bitcast(F16)[:, at:at + P],
                                                         lph[:, t, a, c * P:(c + 1) * P], ident16[:])
                    mm.then_inc(lT_mm, 1)
                if has_b(j, 1):
                    wait(pe, b_xnh, j + 2)
                    wait(pe, b_xnl, j + 2)
                    wait(pe, b_xT_ready, j + 1)
                    for t in range(2):
                        for a in range(2):
                            for k in range(KC):
                                at = (a * KC + k) * P
                                mm = nc.tensor.transpose(bank[:, 4 + t, :].bitcast(F16)[:, at:at + P],
                                                         xnh[:, t, a, k * P:(k + 1) * P], ident16[:])
                    mm.then_inc(b_xT_mm, 1)
                if has_b(j, -1):
                    if isinstance(j, int) and j == 1:
                        pe.wait_ge(hi_set[LV_], 1)
                        pe.wait_ge(lo_set[LV_], 1)
                    wait(pe, lT_ready, j)
                    wait(pe, ob_done, j - 1)
                    for t in range(2):
                        for c in range(LC):
                            for a, w in PASSES:
                                at = ((t * 2 + a) * LC + c) * P
                                mm = nc.tensor.matmul(bank[:, 2 + t, :], lT[:, at:at + P], lv_s[:, w, c, :],
                                                      start=(c == a == w == 0), stop=(c == LC - 1 and w == 1))
                    mm.then_inc(mix_mm, 1)
            iterations_b(pe, body_b)

        @block.vector
        def _(dve):
            steps = [0]

            def scale_of(c, *, also=None):
                if also is not None:
                    nc.vector.tensor_tensor(ar[:, c:c + 1], ar[:, c:c + 1], ar[:, also:also + 1], ALU.max).then_inc(scale_step, 1)
                    steps[0] += 1
                    dve.wait_ge(scale_step, steps[0])
                nc.vector.tensor_scalar(ar[:, c:c + 1], ar[:, c:c + 1], 1e-30, None, ALU.max).then_inc(scale_step, 1)
                dve.wait_ge(scale_step, steps[0] + 1)
                nc.vector.reciprocal(inv[:, c:c + 1], ar[:, c:c + 1]).then_inc(scale_step, 1)
                dve.wait_ge(scale_step, steps[0] + 2)
                nc.vector.tensor_scalar(sc[:, c:c + 1], inv[:, c:c + 1], TARGET, None, ALU.mult).then_inc(scale_step, 1)
                dve.wait_ge(scale_step, steps[0] + 3)
                steps[0] += 3

            nc.vector.memset(am[:], 0.0).then_inc(scale_step, 1)
            steps[0] += 1
            dve.wait_ge(scale_step, 1)
            dve.wait_ge(kf_done, 1)
            nc.vector.tensor_reduce(am[:, K_:K_ + 1], kf[:].rearrange("p c s -> p (c s)"), AX_X, ALU.max,
                                    apply_absolute_value=True).then_inc(absmax_done, 1)
            dve.wait_ge(wq_in, 16)
            nc.vector.tensor_reduce(am[:, WQ_:WQ_ + 1], wq_f[:].rearrange("p c s -> p (c s)"), AX_X, ALU.max,
                                    apply_absolute_value=True).then_inc(absmax_done, 1)
            dve.wait_ge(small_in, 16 * 4)
            nc.vector.tensor_reduce(am[:, 6:7], bq_c[:], AX_X, ALU.max, apply_absolute_value=True).then_inc(absmax_done, 1)
            dve.wait_ge(allmax_done, 1)
            scale_of(K_)
            nc.vector.tensor_scalar(kf[:], kf[:], sc[:, K_:K_ + 1], None, ALU.mult).then_inc(scaled[K_], 1)
            dve.wait_ge(allmax_done, 3)
            scale_of(WQ_, also=6)
            nc.vector.tensor_scalar(bq_c[:], bq_c[:], sc[:, WQ_:WQ_ + 1], None, ALU.mult).then_inc(scale_step, 1)
            steps[0] += 1
            nc.vector.tensor_scalar(wq_f[:], wq_f[:], sc[:, WQ_:WQ_ + 1], None, ALU.mult).then_inc(scaled[WQ_], 1)
            nc.vector.scalar_tensor_tensor(dq[:, DQ_EXP:DQ_EXP + 1], ar[:, WQ_:WQ_ + 1], 1.0 / (TARGET * TARGET * DK ** 0.5),
                                           ar[:, K_:K_ + 1], ALU.mult, ALU.mult).then_inc(scale_step, 1)
            steps[0] += 1
            dve.wait_ge(v_mm, 1)
            nc.vector.tensor_tensor(vf[:], bank[0:S, 2:4, :], bv_r.unsqueeze(1).to_broadcast([S, B, D]),
                                    ALU.add).then_inc(vf_done, 1)
            dve.wait_ge(vf_done, 1)
            nc.vector.tensor_reduce(am[0:S, V_:V_ + 1], vf[:].rearrange("p c s -> p (c s)"), AX_X, ALU.max,
                                    apply_absolute_value=True).then_inc(absmax_done, 1)
            dve.wait_ge(hi_set[K_], 1)
            for r in range(HG):
                rows = slice(r * DK, (r + 1) * DK)
                last = [nc.vector.tensor_tensor(kd[rows, b, 1, :, r * S:(r + 1) * S], kf[rows, :, b * S:(b + 1) * S],
                                                kd[rows, b, 0, :, r * S:(r + 1) * S], ALU.subtract) for b in range(B)][-1]
            last.then_inc(lo_set[K_], 1)
            dve.wait_ge(hi_set[WQ_], 1)
            nc.vector.tensor_tensor(wq_s[:, 1], wq_f[:], wq_s[:, 0], ALU.subtract).then_inc(lo_set[WQ_], 1)

            def stats(i, par):
                wait(dve, x_here, x_quarter(i))
                wait(dve, rstd_done, i)
                nc.vector.bn_stats(st6[:, 0, :], tile_of_x(i)).then_inc(stats_done, 1)

            def aggregate(i):
                if isinstance(i, int):
                    wait(dve, stats_done, i + 1)
                nc.vector.bn_aggr(mv[:, 0, :], st6[:, 0, :]).then_inc(aggr_done, 1)

            def x_quarter(i):
                return i // XQ + 1 if isinstance(i, int) else NQ

            def normalise(i):
                wait(dve, rstd_done, i + 1)
                wait(dve, xnl_done, i)
                nc.vector.tensor_scalar(xn[:, 0, :], tile_of_x(i), mv[:, 0, 0:1], rstd[:, 0:1], ALU.subtract,
                                        ALU.mult).then_inc(xn_done, 1)

            def max_sub(i, g):
                n = 4 * i + g
                sv = s_bank(g % 2).rearrange("p (h s) -> p h s", h=HG)
                wait(dve, s_mm, n + 1)
                nc.vector.tensor_reduce(mx[:, g % 2, :], sv, AX_X, ALU.max).then_inc(max_done, 1)
                wait(dve, max_done, n + 1)
                wait(dve, exp_done, n - 1)
                if g == 0 and has(i, 2):
                    wait(dve, stats_done, i + 3)
                nc.vector.tensor_tensor(df[:, g % 2, :].rearrange("p (h s) -> p h s", h=HG), sv,
                                        mx[:, g % 2, :].unsqueeze(2).to_broadcast([P, HG, S]), ALU.subtract).then_inc(sub_done, 1)

            def probs_low(i, g):
                n = 4 * i + g
                wait(dve, pTh_done, n + 1)
                nc.vector.tensor_tensor(pT[0:CR, g % 2, 1, :], pT_bank(g % 2), pT[0:CR, g % 2, 0, :],
                                        ALU.subtract).then_inc(pTl_done, 1)

            def context(i, half):
                n = 2 * i + half
                o = o_bank(half).rearrange("p (h v) -> p h v", v=VW)
                wait(dve, pv_mm, 2 * n + 2)
                nc.vector.reciprocal(rden[:, half, :], o[:, :, DK]).then_inc(rden_done, 1)
                wait(dve, rden_done, n + 1)
                wait(dve, cxl_done, n - 1)
                nc.vector.tensor_tensor(cx[:, half * (D // 2):(half + 1) * (D // 2)].rearrange("p (h v) -> p h v", v=DK),
                                        o[:, :, 0:DK], rden[:, half, :].unsqueeze(2).to_broadcast([P, H // 2, DK]),
                                        ALU.mult).then_inc(cx_done, 1)

            def q_low(i, par):
                wait(dve, qh_done, i + 1)
                for m in range(KC):
                    last = nc.vector.scalar_tensor_tensor(qT[:, par, 1, m, :], qw_bank[:, m * P:(m + 1) * P], bq_c[:, m:m + 1],
                                                          qT[:, par, 0, m, :], ALU.add, ALU.subtract)
                last.then_inc(ql_done, 1)

            def residual(i):
                wait(dve, wo_mm, i + 1)
                wait(dve, xb_done, i + 1)
                nc.vector.scalar_tensor_tensor(tile_of_x(i), qw_bank, dq[:, DQ_OUT:DQ_OUT + 1], tile_of_x(i),
                                               ALU.mult, ALU.add).then_inc(x2_done, 1)

            def v_and_wo():
                dve.wait_ge(allmax_done, 4)
                scale_of(V_)
                nc.vector.tensor_scalar(vf[:], vf[:], sc[0:S, V_:V_ + 1], None, ALU.mult).then_inc(scaled[V_], 1)
                dve.wait_ge(hi_set[V_], 1)
                nc.vector.tensor_tensor(vh[:, :, 1, :], vf[:], vh[:, :, 0, :], ALU.subtract).then_inc(lo_set[V_], 1)
                dve.wait_ge(wo_in, 16)
                nc.vector.tensor_reduce(am[:, WO_:WO_ + 1], wo_f[:].rearrange("p c s -> p (c s)"), AX_X, ALU.max,
                                        apply_absolute_value=True).then_inc(absmax_done, 1)
                dve.wait_ge(allmax_done, 5)
                scale_of(WO_)
                nc.vector.tensor_scalar(wo_f[:], wo_f[:], sc[:, WO_:WO_ + 1], None, ALU.mult).then_inc(scaled[WO_], 1)
                nc.vector.scalar_tensor_tensor(dq[:, DQ_OUT:DQ_OUT + 1], ar[:, V_:V_ + 1], 1.0 / (TARGET * TARGET),
                                               ar[:, WO_:WO_ + 1], ALU.mult, ALU.mult).then_inc(scale_step, 1)
                steps[0] += 1
                dve.wait_ge(hi_set[WO_], 1)
                nc.vector.tensor_tensor(wo_s[:, 1], wo_f[:], wo_s[:, 0], ALU.subtract).then_inc(lo_set[WO_], 1)

            def body(i, par, b, b_before):
                if isinstance(i, int) and i == 0:
                    v_and_wo()
                for g in range(NG):
                    if g == 0 and has(i, 2):
                        stats(i + 2, par)
                    if has(i, 0):
                        max_sub(i, g)
                    if g == 0 and has(i, 2):
                        aggregate(i + 2)
                    if g == 1 and has(i, -2):
                        residual(i - 2)
                    if g == 3 and has(i, 1):
                        q_low(i + 1, 1 - par)
                    if g == 0 and has(i, -1):
                        probs_low(i - 1, 3)
                    if g > 0 and has(i, 0):
                        probs_low(i, g - 1)
                    if g == 1 and has(i, -1):
                        context(i - 1, 1)
                    if g == 3 and has(i, 0):
                        context(i, 0)
                    if g == 2 and has(i, 2):
                        normalise(i + 2)

            iterations_a(dve, body)

            dve.wait_ge(g_mm, 1)
            gv = bank[:, 0:2, :].rearrange("p a (m n) -> p (a m) n", m=2)[:, :, 0:NI]
            nc.vector.tensor_reduce(am[:, G_:G_ + 1], gv, mybir.AxisListType.XY, ALU.max,
                                    apply_absolute_value=True).then_inc(absmax_done, 1)
            dve.wait_ge(allmax_done, 6)
            scale_of(G_)
            nc.vector.tensor_scalar(fq_f[:, :, 0:NI], gv, sc[:, G_:G_ + 1], None, ALU.mult).then_inc(scaled[G_], 1)
            nc.vector.tensor_scalar(dq[:, DQ_TANH:DQ_TANH + 1], ar[:, G_:G_ + 1], 0.5 / TARGET, None, ALU.mult).then_inc(scale_step, 1)
            steps[0] += 1
            dve.wait_ge(hi_set[G_], 1)
            nc.vector.tensor_tensor(g_s[:, 1, :, 0:NI], fq_f[:, :, 0:NI], g_s[:, 0, :, 0:NI], ALU.subtract).then_inc(lo_set[G_], 1)

            def leaf_values():
                dve.wait_ge(lv_mm, 1)
                nc.vector.tensor_reduce(am[:, LV_:LV_ + 1], bank[:, 2:4, :], mybir.AxisListType.XY, ALU.max,
                                        apply_absolute_value=True).then_inc(absmax_done, 1)
                dve.wait_ge(allmax_done, 7)
                scale_of(LV_)
                nc.vector.tensor_scalar(wout_f[:, 0:LC, :], bank[:, 2:4, :], sc[:, LV_:LV_ + 1], None, ALU.mult).then_inc(scaled[LV_], 1)
                nc.vector.tensor_scalar(dq[:, DQ_MIX:DQ_MIX + 1], ar[:, LV_:LV_ + 1], 1.0 / (TARGET * ROOT), None,
                                        ALU.mult).then_inc(scale_step, 1)
                steps[0] += 1
                dve.wait_ge(hi_set[LV_], 1)
                nc.vector.tensor_tensor(lv_s[:, 1], wout_f[:, 0:LC, :], lv_s[:, 0], ALU.subtract).then_inc(lo_set[LV_], 1)

            def body_b(j, par, q):
                if has_b(j, 1):
                    wait(dve, b_rstd, j + 2)
                    wait(dve, b_xnl, j + 1)
                    for t in range(2):
                        nc.vector.tensor_scalar(xn[:, t, :], tile_of_x(2 * j + 2 + t), mv[:, t, 0:1], rstd[:, t:t + 1],
                                                ALU.subtract, ALU.mult).then_inc(b_xn, 1)
                if has_b(j, 0):
                    wait(dve, fr_done, 2 * j + 2)
                    nc.vector.tensor_scalar(lp[0][:, :, 0:2], fr[:, :, :, 0], ROOT, None, ALU.mult).then_inc(lvl_done, 1)
                    for lv in range(1, DEPTH):
                        n = 2 ** lv
                        wait(dve, lvl_done, DEPTH * j + lv)
                        if lv == DEPTH - 1:
                            wait(dve, lpl_done, j)
                        dst, src = lp[lv % 2], lp[1 - lv % 2]
                        for t in range(2):
                            last = nc.vector.tensor_tensor(dst[:, t, 0:2 * n].rearrange("p (n s) -> p n s", s=2),
                                                           src[:, t, 0:n].unsqueeze(2).to_broadcast([P, n, 2]),
                                                           fr[:, t, :, n - 1:2 * n - 1].rearrange("p s n -> p n s"), ALU.mult)
                        last.then_inc(lvl_done, 1)
                if has_b(j, -1):
                    if isinstance(j, int) and j == 1:
                        pass
                    wait(dve, mix_mm, j)
                    wait(dve, b_xb, j)
                    jq, jp = (q, 0) if par else (q - 1, 1)
                    wait(dve, stored[jp], 16 * jq)
                    for t in range(2):
                        last = nc.vector.scalar_tensor_tensor(ob[:, jp, t, :], bank[:, 2 + t, :], dq[:, DQ_MIX:DQ_MIX + 1],
                                                              tile_of_x(2 * j - 2 + t), ALU.mult, ALU.add)
                    last.then_inc(ob_done, 1)
                if has_b(j, 2):
                    for t in range(2):
                        nc.vector.bn_stats(st6[:, t, :], tile_of_x(2 * j + 4 + t)).then_inc(b_stats, 1)
                    if not has_b(j, 0) or isinstance(j, int):
                        wait(dve, b_stats, 2 * j + 6)
                if has_b(j, 0):
                    if has_b(j, 2):
                        wait(dve, b_stats, 2 * j + 6)
                    wait(dve, lph_done, j + 1)
                    nc.vector.tensor_tensor(lph[:, :, 1, :], lp[1], lph[:, :, 0, :], ALU.subtract).then_inc(lpl_done, 1)
                if has_b(j, 2):
                    for t in range(2):
                        nc.vector.bn_aggr(mv[:, t, :], st6[:, t, :]).then_inc(b_aggr, 1)
                if isinstance(j, int) and j == -1:
                    leaf_values()
            iterations_b(dve, body_b)

        @block.scalar
        def _(act):
            act.dma_start(wq_f[:], chunked(W_Q)).then_inc(wq_in, 16)
            act.dma_start(bk_c[:], b_K).then_inc(small_in, 16)
            act.dma_start(bq_c[:], b_Q).then_inc(small_in, 16)
            act.dma_start(bv_r, b_V.partition_broadcast(S)).then_inc(small_in, 16)
            act.dma_start(oc[:], ones_cols).then_inc(small_in, 16)
            act.dma_start(ident[:], eye).then_inc(consts_set, 16)
            act.dma_start(ident16[:], eye16).then_inc(consts_set, 16)
            act.dma_start(wo_f[:], chunked(W_O)).then_inc(wo_in, 16)
            act.dma_start(bo_r[:], b_O.partition_broadcast(P)).then_inc(late_in, 16)
            act.dma_start(bout_r[:], Wout_b.partition_broadcast(P)).then_inc(late_in, 16)
            act.wait_ge(small_in, 16 * 4)
            act.wait_ge(k_mm, 1)
            for m in range(KC):
                last = nc.scalar.activation(kf[:, m, :], bank[:, m // 2, (m % 2) * B * S:(m % 2 + 1) * B * S],
                                            ACT.Identity, bias=bk_c[:, m:m + 1])
            last.then_inc(kf_done, 1)
            act.wait_ge(scaled[K_], 1)
            act.wait_ge(kd_zero, 1)
            for r in range(HG):
                rows = slice(r * DK, (r + 1) * DK)
                last = [nc.scalar.activation(kd[rows, b, 0, :, r * S:(r + 1) * S], kf[rows, :, b * S:(b + 1) * S], ACT.Copy)
                        for b in range(B)][-1]
            last.then_inc(hi_set[K_], 1)
            act.wait_ge(scaled[WQ_], 1)
            nc.scalar.activation(wq_s[:, 0], wq_f[:], ACT.Copy).then_inc(hi_set[WQ_], 1)

            def x_high(i):
                wait(act, xn_done, i + 1)
                wait(act, xT_mm, i)
                nc.scalar.activation(xnh[:, 0, 0, :], xn[:, 0, :], ACT.Copy).then_inc(xnh_done, 1)

            def x_T_out(i):
                wait(act, xT_mm, i + 1)
                wait(act, q_mm, i)
                nc.scalar.activation(xT[:, 0, :].bitcast(F32), tr_bank.bitcast(F32), ACT.Copy).then_inc(xT_ready, 1)

            def q_high(i, par):
                wait(act, q_mm, i + 1)
                wait(act, s_mm, 4 * (i - 1))
                for m in range(KC):
                    last = nc.scalar.activation(qT[:, par, 0, m, :], qw_bank[:, m * P:(m + 1) * P], ACT.Identity, bias=bq_c[:, m:m + 1])
                last.then_inc(qh_done, 1)

            def exp(i, g):
                n = 4 * i + g
                wait(act, sub_done, n + 1)
                wait(act, pT_mm, n - 1)
                nc.scalar.activation(pr[:, g % 2, 0:GS], df[:, g % 2, :], ACT.Exp, scale=dq[:, DQ_EXP:DQ_EXP + 1]).then_inc(exp_done, 1)

            def probs_high(i, g):
                n = 4 * i + g
                wait(act, pT_mm, n + 1)
                wait(act, pv_mm, n - 1)
                nc.scalar.activation(pT[0:CR, g % 2, 0, :], pT_bank(g % 2), ACT.Copy).then_inc(pTh_done, 1)

            def ctx_high(i, half):
                cols = slice(half * (D // 2), (half + 1) * (D // 2))
                wait(act, cx_done, 2 * i + half + 1)
                wait(act, cxT_mm, i)
                nc.scalar.activation(cxh[:, 0, cols], cx[:, cols], ACT.Copy).then_inc(cxh_done, 1)

            def ctx_T_out(i):
                wait(act, cxT_mm, i + 1)
                wait(act, wo_mm, i)
                nc.scalar.activation(cxT.bitcast(F32), tr_bank.bitcast(F32), ACT.Copy).then_inc(cxT_ready, 1)

            def body(i, par, b, b_before):
                if isinstance(i, int) and i == 0:
                    act.wait_ge(scaled[V_], 1)
                    nc.scalar.activation(vh[:, :, 0, :], vf[:], ACT.Copy).then_inc(hi_set[V_], 1)
                    act.wait_ge(scaled[WO_], 1)
                    nc.scalar.activation(wo_s[:, 0], wo_f[:], ACT.Copy).then_inc(hi_set[WO_], 1)
                for g in range(NG):
                    if g == 0 and has(i, -1):
                        ctx_high(i - 1, 0)
                    if g == 1 and has(i, 1):
                        x_T_out(i + 1)
                    if g == 2 and has(i, -1):
                        ctx_high(i - 1, 1)
                    if g == 3 and has(i, 1):
                        q_high(i + 1, 1 - par)
                    if g == 3 and has(i, -1):
                        ctx_T_out(i - 1)
                    if g == 0 and has(i, -1):
                        probs_high(i - 1, 3)
                    if g > 0 and has(i, 0):
                        probs_high(i, g - 1)
                    if has(i, 0):
                        exp(i, g)
                    if g == 3 and has(i, 2):
                        x_high(i + 2)
            iterations_a(act, body)

            act.wait_ge(scaled[G_], 1)
            nc.scalar.activation(g_s[:, 0, :, 0:NI], fq_f[:, :, 0:NI], ACT.Copy).then_inc(hi_set[G_], 1)

            def body_b(j, par, q):
                if has_b(j, 0):
                    wait(act, lg_mm, j + 1)
                    wait(act, fr_done, 2 * j)
                    nc.scalar.activation(th, bank[:, 6 + par, :].rearrange("p (t n) -> p t n", t=2)[:, :, 0:NI], ACT.Tanh,
                                         scale=dq[:, DQ_TANH:DQ_TANH + 1]).then_inc(th_done, 1)
                    wait(act, th_done, j + 1)
                    wait(act, lvl_done, DEPTH * j)
                    nc.scalar.activation(fr[:, :, 0, :], th, ACT.Copy, bias=0.5, scale=-0.5).then_inc(fr_done, 1)
                    nc.scalar.activation(fr[:, :, 1, :], th, ACT.Copy, bias=0.5, scale=0.5).then_inc(fr_done, 1)
                if has_b(j, -1):
                    wait(act, lT_mm, j)
                    wait(act, mix_mm, j - 1)
                    nc.scalar.activation(lT.bitcast(F32), bank[:, 0, :], ACT.Copy).then_inc(lT_ready, 1)
                if has_b(j, 1):
                    wait(act, b_xn, 2 * j + 4)
                    wait(act, b_xT_mm, j + 1)
                    nc.scalar.activation(xnh[:, :, 0, :], xn[:], ACT.Copy).then_inc(b_xnh, 1)
                    wait(act, b_xT_mm, j + 2)
                    wait(act, lg_mm, j + 1)
                    nc.scalar.activation(xT[:].bitcast(F32), bank[:, 4:6, :], ACT.Copy).then_inc(b_xT_ready, 1)
                if has_b(j, 0):
                    wait(act, lvl_done, DEPTH * (j + 1))
                    wait(act, lT_mm, j)
                    nc.scalar.activation(lph[:, :, 0, :], lp[1], ACT.Copy).then_inc(lph_done, 1)
                if isinstance(j, int) and j == -1:
                    act.wait_ge(scaled[LV_], 1)
                    nc.scalar.activation(lv_s[:, 0], wout_f[:, 0:LC, :], ACT.Copy).then_inc(hi_set[LV_], 1)
            iterations_b(act, body_b)

        @block.gpsimd
        def _(pool):
            pool.dma_start(fq_f[:], chunked(Wq)).then_inc(fq_in, 16)
            pool.dma_start(rt_f[:], chunked(routersT)).then_inc(rt_in, 16)
            pool.dma_start(wout_f[:], chunked(WoutT)).then_inc(wout_in, 16)
            pool.dma_start(lf_f[:], chunked(leafvT)).then_inc(lf_in, 16)
            nc.gpsimd.memset(kd[:], 0.0).then_inc(kd_zero, 1)
            nc.gpsimd.memset(vd[:], 0.0).then_inc(vd_zero, 1)
            nc.gpsimd.memset(pr[:, :, GS:RC * CR], 0.0).then_inc(vd_zero, 1)
            nc.gpsimd.memset(mhalf[:], -0.5).then_inc(vd_zero, 1)
            nc.gpsimd.memset(eps[:], EPS).then_inc(vd_zero, 1)

            def all_max(col, count):
                pool.wait_ge(absmax_done, count)
                nc.gpsimd.partition_all_reduce(ar[:, col:col + 1], am[:, col:col + 1], P, RMAX).then_inc(allmax_done, 1)

            for count, col in enumerate((K_, WQ_, 6, V_)):
                all_max(col, count + 1)
            pool.wait_ge(small_in, 16 * 4)
            pool.wait_ge(vd_zero, 4)
            for c in range(RC):
                for b in range(B):
                    last = nc.gpsimd.tensor_copy(vd[:, c, b, 0, :, :, DK], oc[:, c, :].unsqueeze(1).to_broadcast([P, NG, 2]))
            last.then_inc(vd_ones, 1)

            def place_v():
                pool.wait_ge(hi_set[V_], 1)
                pool.wait_ge(lo_set[V_], 1)
                pool.wait_ge(vd_ones, 1)
                for hh in range(HG):
                    s0 = 0
                    while s0 < S:
                        row = hh * S + s0
                        c = row // CR
                        n = min(S - s0, (c + 1) * CR - row)
                        for b in range(B):
                            pass
                        yield hh, s0, n, c, row - c * CR
                        s0 += n

            def rstd_of(i):
                wait(pool, aggr_done, i + 1)
                nc.gpsimd.tensor_tensor(veps[:, 0:1], mv[:, 0, 1:2], eps[:, 0:1], ALU.add).then_inc(veps_done, 1)
                wait(pool, veps_done, i + 1)
                nc.gpsimd.tensor_tensor(rstd[:, 0:1], veps[:, 0:1], mhalf[:, 0:1], ALU.pow).then_inc(rstd_done, 1)

            def x_low(i):
                wait(pool, xnh_done, i + 1)
                nc.gpsimd.tensor_tensor(xnh[:, 0, 1, :], xn[:, 0, :], xnh[:, 0, 0, :], ALU.subtract).then_inc(xnl_done, 1)

            def x_bias(i):
                wait(pool, xn_done, i + 1)
                nc.gpsimd.tensor_tensor(tile_of_x(i), tile_of_x(i), bo_r[:], ALU.add).then_inc(xb_done, 1)

            def ctx_low(i, half):
                cols = slice(half * (D // 2), (half + 1) * (D // 2))
                wait(pool, cxh_done, 2 * i + half + 1)
                nc.gpsimd.tensor_tensor(cxh[:, 1, cols], cx[:, cols], cxh[:, 0, cols], ALU.subtract).then_inc(cxl_done, 1)

            def body(i, par, b, b_before):
                if isinstance(i, int) and i == -2:
                    pool.wait_ge(late_in, 32)
                if isinstance(i, int) and i == 0:
                    for hh, s0, n, c, row in place_v():
                        pool.dma_start(vd[row:row + n, c, :, :, :, hh - c, 0:DK].rearrange("p b a g v -> p (b a) g v"),
                                       vh[s0:s0 + n, :, :, :].rearrange("p b a (g h v) -> p (b a) g h v", g=NG, h=HG)[:, :, :, hh, :]
                                       ).then_inc(vd_in, 16)
                    all_max(WO_, 5)
                if has(i, -1):
                    ctx_low(i - 1, 0)
                if has(i, 2):
                    rstd_of(i + 2)
                if has(i, -1):
                    ctx_low(i - 1, 1)
                if has(i, 2):
                    x_low(i + 2)
                    x_bias(i + 2)
            iterations_a(pool, body)
            all_max(G_, 6)

            def body_b(j, par, q):
                if has_b(j, 1):
                    wait(pool, b_aggr, 2 * j + 4)
                    nc.gpsimd.tensor_tensor(veps[:], mv[:, :, 1], eps[:], ALU.add).then_inc(b_veps, 1)
                    wait(pool, b_veps, j + 2)
                    nc.gpsimd.tensor_tensor(rstd[:], veps[:], mhalf[:], ALU.pow).then_inc(b_rstd, 1)
                    wait(pool, b_xnh, j + 2)
                    nc.gpsimd.tensor_tensor(xnh[:, :, 1, :], xn[:], xnh[:, :, 0, :], ALU.subtract).then_inc(b_xnl, 1)
                if isinstance(j, int) and j == -1:
                    all_max(LV_, 7)
                if has_b(j, 1):
                    for t in range(2):
                        last = nc.gpsimd.tensor_tensor(tile_of_x(2 * j + 2 + t), tile_of_x(2 * j + 2 + t), bout_r[:], ALU.add)
                    last.then_inc(b_xb, 1)
            iterations_b(pool, body_b)


def kernel(**inputs):
    import concourse.bacc as bacc
    from concourse.bass_utils import run_bass_kernel_spmd

    a = {k: np.asarray(v) for k, v in inputs.items()}
    p = "L0_xattn_"
    f = "L0_ffn_"
    ones_cols = np.zeros((P, RC, 2), np.float16)
    for row in range(GS):
        c = row // CR
        ones_cols[row - c * CR, c, row // S - c] = 1.0
    arrays = {
        "x": a["x"], "ctxT": a["ctx_1024"].reshape(B * S, D).T,
        "W_Q": a[p + "W_Q"], "b_Q": a[p + "b_Q"].reshape(KC, P).T, "W_K": a[p + "W_K"], "b_K": a[p + "b_K"].reshape(KC, P).T,
        "W_V": a[p + "W_V"], "b_V": a[p + "b_V"], "W_O": a[p + "W_O"], "b_O": a[p + "b_O"],
        "Wq": a[f + "Wq"], "routersT": a[f + "routers"].T, "leafvT": a[f + "leaf_values"].T,
        "WoutT": a[f + "Wout_w"].T, "Wout_b": a[f + "Wout_b"],
        "eye": np.eye(P, dtype=np.float32), "eye16": np.eye(P, dtype=np.float16), "ones_cols": ones_cols,
    }
    arrays = {k: np.ascontiguousarray(v) for k, v in arrays.items()}
    nc = bacc.Bacc("TRN2", target_bir_lowering=False, num_devices=1)
    args = {k: nc.dram_tensor(f"in_{k}", v.shape, mybir.dt.from_np(v.dtype), kind="ExternalInput").ap() for k, v in arrays.items()}
    out = nc.dram_tensor("out_x", (B, L, D), F32, kind="ExternalOutput").ap()
    build(nc, out=out, **args)
    r = run_bass_kernel_spmd(nc, [{f"in_{k}": v for k, v in arrays.items()}], core_ids=[0])
    return r.results[0]["out_x"]
```

```python
from contextlib import ExitStack

import numpy as np

import concourse.bass as bass
from concourse import mybir

F32 = mybir.dt.float32
F16 = mybir.dt.float16
ALU = mybir.AluOpType
ACT = mybir.ActivationFunctionType
AX_X = mybir.AxisListType.X
RMAX = bass.bass_isa.ReduceOp.max

P = 128
B, L, S, D = 2, 2048, 77, 512
H, DK = 16, 32
KC = D // P
NT = B * L // P
TPB = NT // B
XQ = 4
NQ = NT // XQ
HG = P // DK
NG = H // HG
GS = HG * S
RC = 3
CR = -(-GS // RC)
VW = DK + 1
DEPTH = 8
M = 2 ** DEPTH
NI = M - 1
LC = M // P
NP = NT // 2
TARGET = 64.0
ROOT = 2.0 ** 15
EPS = 1e-5
PASSES = [(0, 0), (1, 0), (0, 1)]


def build(nc, x, ctxT, W_Q, b_Q, W_K, b_K, W_V, b_V, W_O, b_O, Wq, routersT, leafvT, WoutT, Wout_b,
          eye, eye16, ones_cols, out):
    ctx = ExitStack()
    with ctx:
        def sb(name, shape, dt=F32):
            return ctx.enter_context(nc.sbuf_tensor(name, shape, dt))

        def sem(name):
            return ctx.enter_context(nc.semaphore(name))

        xs = sb("xs", [P, NT * D])
        ident = sb("ident", [P, P])
        ident16 = sb("ident16", [P, P], F16)
        wq_f = sb("wq_f", [P, KC, D])
        wk_f = sb("wk_f", [P, KC, D])
        wv_f = sb("wv_f", [P, KC, D])
        wo_f = sb("wo_f", [P, KC, D])
        fq_f = sb("fq_f", [P, KC, D])
        wout_f = sb("wout_f", [P, KC, D])
        rt_f = sb("rt_f", [P, KC, NI])
        lf_f = sb("lf_f", [P, KC, M])
        cT = sb("cT", [P, KC, B * S])
        bq_c = sb("bq_c", [P, KC])
        bk_c = sb("bk_c", [P, KC])
        bv_room = sb("bv_room", [P, D])
        bv_r = bv_room[0:S]
        bo_r = sb("bo_r", [P, D])
        bout_r = sb("bout_r", [P, D])
        wq_s = sb("wq_s", [P, 2, KC, D], F16)
        wo_s = sb("wo_s", [P, 2, KC, D], F16)
        g_s = sb("g_s", [P, 2, KC, NI + 1], F16)
        lv_s = sb("lv_s", [P, 2, LC, D], F16)
        kf = sb("kf", [P, KC, B * S])
        kd = sb("kd", [P, B, 2, NG, GS], F16)
        vf = sb("vf", [S, B, D])
        v_room = sb("v_room", [P, B, 2, D], F16)
        vh = v_room[0:S]
        vd = sb("vd", [P, RC, B, 2, NG, 2, VW], F16)
        oc = sb("oc", [P, RC, 2], F16)
        am = sb("am", [P, 8])
        ar = sb("ar", [P, 8])
        sc = sb("sc", [P, 8])
        dq = sb("dq", [P, 8])
        st6 = sb("st6", [P, 2, 6])
        mv = sb("mv", [P, 2, 2])
        veps = sb("veps", [P, 2])
        mhalf = sb("mhalf", [P, 2])
        eps = sb("eps", [P, 2])
        rstd = sb("rstd", [P, 2])
        xn = sb("xn", [P, 2, D])
        xnh = sb("xnh", [P, 2, 2, D], F16)
        xT = sb("xT", [P, 2, 2 * KC * P], F16)
        qf = cT[:].rearrange("p c s -> p (c s)")[:, 0:D].rearrange("p (c t) -> p c t", c=KC)
        qT = sb("qT", [P, 2, 2, KC, P], F16)
        mx = sb("mx", [P, 2, HG])
        df = sb("df", [P, 2, GS])
        pr = sb("pr", [P, 2, RC * CR])
        pT = sb("pT", [P, 2, 2, RC * P], F16)
        rden = sb("rden", [P, 2, H // 2])
        cx = sb("cx", [P, D])
        cxh = sb("cxh", [P, 2, D], F16)
        cxT = v_room[:, 0].rearrange("p a n -> p (a n)")
        lT = v_room[:, 1].rearrange("p a n -> p (a n)")
        lph = bv_room[:].bitcast(F16).rearrange("p (t a m) -> p t a m", t=2, a=2)
        ob = wk_f[:].rearrange("p (a t) n -> p a t n", a=2)
        wv_room = wv_f[:].rearrange("p c n -> p (c n)")
        lp = [wv_room[:, n * 2 * M:(n + 1) * 2 * M].rearrange("p (t m) -> p t m", t=2) for n in range(2)]
        fr = wv_room[:, 4 * M:4 * M + 4 * NI].rearrange("p (t s n) -> p t s n", t=2, s=2)
        th = kf[:].rearrange("p c s -> p (c s)")[:, 0:2 * NI].rearrange("p (t n) -> p t n", t=2)
        gf = fq_f[:, :, 0:NI]
        bank = ctx.enter_context(nc.psum_tensor("bank", [P, 8, 512], F32))

        def tile_of_x(i):
            return xs[:, bass.ds(i * D, D)]

        small_in, cT_in, wk_in, wq_in, wv_in, wo_in = (sem(n) for n in (
            "small_in", "cT_in", "wk_in", "wq_in", "wv_in", "wo_in"))
        fq_in, rt_in, wout_in, lf_in, late_in = (sem(n) for n in ("fq_in", "rt_in", "wout_in", "lf_in", "late_in"))
        x_in = [sem(f"x_in{q}") for q in range(NQ)]
        x_here = sem("x_here")
        consts_set = sem("consts_set")
        k_mm, v_mm, g_mm, lv_mm = (sem(n) for n in ("k_mm", "v_mm", "g_mm", "lv_mm"))
        kf_done, vf_done = sem("kf_done"), sem("vf_done")
        absmax_done, allmax_done, scale_step = sem("absmax_done"), sem("allmax_done"), sem("scale_step")
        scaled = [sem(f"scaled{n}") for n in range(6)]
        hi_set = [sem(f"hi_set{n}") for n in range(6)]
        lo_set = [sem(f"lo_set{n}") for n in range(6)]
        scale_set = [sem(f"scale_set{n}") for n in range(6)]
        bq_scaled, gf_done, dq_set = sem("bq_scaled"), sem("gf_done"), sem("dq_set")
        vd_zero, vd_ones, vd_in = sem("vd_zero"), sem("vd_ones"), sem("vd_in")
        kd_zero = sem("kd_zero")
        stats_done, aggr_done, veps_done, rstd_done, xn_done, xnh_done, xnl_done, xb_done = (sem(n) for n in (
            "stats_done", "aggr_done", "veps_done", "rstd_done", "xn_done", "xnh_done", "xnl_done", "xb_done"))
        xT_mm, xT_ready, q_mm, qf_done, qh_done, ql_done = (sem(n) for n in (
            "xT_mm", "xT_ready", "q_mm", "qf_done", "qh_done", "ql_done"))
        s_mm, max_done, sub_done, exp_done, pT_mm, pTh_done, pTl_done, pv_mm = (sem(n) for n in (
            "s_mm", "max_done", "sub_done", "exp_done", "pT_mm", "pTh_done", "pTl_done", "pv_mm"))
        rden_done, cx_done, cxh_done, cxl_done, cxT_mm, cxT_ready, wo_mm, x2_done = (sem(n) for n in (
            "rden_done", "cx_done", "cxh_done", "cxl_done", "cxT_mm", "cxT_ready", "wo_mm", "x2_done"))
        b_stats, b_aggr, b_veps, b_rstd, b_xn, b_xnh, b_xnl, b_xb = (sem(n) for n in (
            "b_stats", "b_aggr", "b_veps", "b_rstd", "b_xn", "b_xnh", "b_xnl", "b_xb"))
        b_xT_mm, b_xT_ready, lg_mm, th_done, fr_done, lvl_done, lph_done, lpl_done = (sem(n) for n in (
            "b_xT_mm", "b_xT_ready", "lg_mm", "th_done", "fr_done", "lvl_done", "lph_done", "lpl_done"))
        lT_mm, lT_ready, mix_mm, ob_done = (sem(n) for n in ("lT_mm", "lT_ready", "mix_mm", "ob_done"))
        stored = [sem("stored0"), sem("stored1")]

        def wait(eng, s, v):
            if not isinstance(v, int) or v > 0:
                eng.wait_ge(s, v)

        WQ_, K_, V_, WO_, G_, LV_ = range(6)
        DQ_EXP, DQ_OUT, DQ_TANH, DQ_MIX = range(4)

        x_v = x.rearrange("b (q p t) d -> (b q) p (t d)", p=P, t=XQ)
        out_v = out.rearrange("b (q p t) d -> (b q) p (t d)", p=P, t=XQ)

        def chunked(w):
            return w.rearrange("(c p) n -> p c n", p=P)

        def s_bank(n2):
            return bank[:, n2, 0:GS]

        def pT_bank(n2):
            return bank[0:CR, 2 + n2, 0:RC * P]

        def o_bank(half):
            return bank[:, 4 + half, 0:H // 2 * VW]

        tr_bank = bank[:, 6, :].bitcast(F16)
        qw_bank = bank[:, 7, :]

        def iterations_a(eng, body, body_b):
            for i in range(-2, 2):
                body(i, i % 2, 0, 0)
            with eng.Fori(1, TPB // 2) as j:
                for par in range(2):
                    body(2 * j + par, par, 0, 0)
            for par in range(2):
                body(TPB + par, par, 1, par)
            with eng.Fori(TPB // 2 + 1, NT // 2 - 1) as j:
                for par in range(2):
                    body(2 * j + par, par, 1, 1)
            for i in range(NT - 2, NT):
                body(i, i % 2, 1, 1)
            for j in range(-2, 0):
                body_b(j, j % 2, j // 2)
            for i in range(NT, NT + 2):
                body(i, i % 2, 1, 1)
            body_b(0, 0, 0)

        def has(i, *offs):
            return not isinstance(i, int) or all(0 <= i + o < NT for o in offs)

        def iterations_b(eng, body):
            for j in range(1, 4):
                body(j, j % 2, j // 2)
            with eng.Fori(2, NQ - 1) as q:
                for par in range(2):
                    body(2 * q + par, par, q)
            for j in range(NP - 2, NP + 3):
                body(j, j % 2, j // 2)

        def has_b(j, *offs):
            return not isinstance(j, int) or all(0 <= j + o < NP for o in offs)

        block = ctx.enter_context(nc.Block())

        @block.sync
        def _(sp):
            sp.dma_start(cT[:], chunked(ctxT)).then_inc(cT_in, 16)
            sp.dma_start(wk_f[:], chunked(W_K)).then_inc(wk_in, 16)
            sp.dma_start(wq_f[:], chunked(W_Q)).then_inc(wq_in, 16)
            sp.dma_start(xs[:, 0:XQ * D], x_v[0]).then_inc(x_in[0], 16)
            sp.dma_start(wv_f[:], chunked(W_V)).then_inc(wv_in, 16)
            sp.dma_start(fq_f[:], chunked(Wq)).then_inc(fq_in, 16)
            sp.dma_start(rt_f[:], chunked(routersT)).then_inc(rt_in, 16)
            sp.dma_start(wo_f[:], chunked(W_O)).then_inc(wo_in, 16)
            sp.dma_start(xs[:, XQ * D:2 * XQ * D], x_v[1]).then_inc(x_in[1], 16)
            sp.dma_start(wout_f[:], chunked(WoutT)).then_inc(wout_in, 16)
            sp.dma_start(lf_f[:], chunked(leafvT)).then_inc(lf_in, 16)
            for q in range(2, NQ):
                sp.dma_start(xs[:, q * XQ * D:(q + 1) * XQ * D], x_v[q]).then_inc(x_in[q], 16)
            sp.wait_ge(x_in[0], 16)
            sp.sem_inc(x_here, 1)
            sp.wait_ge(hi_set[V_], 1)
            sp.wait_ge(lo_set[V_], 1)
            sp.wait_ge(vd_ones, 1)
            for hh in range(HG):
                s0 = 0
                while s0 < S:
                    c, row = divmod(hh * S + s0, CR)
                    n = min(S - s0, CR - row)
                    sp.dma_start(vd[row:row + n, c, :, :, :, hh - c, 0:DK].rearrange("p b a g v -> p (b a) g v"),
                                 vh[s0:s0 + n, :, :, :].rearrange("p b a (g h v) -> p (b a) g h v", g=NG, h=HG)[:, :, :, hh, :]
                                 ).then_inc(vd_in, 16)
                    s0 += n
            for q in range(1, NQ):
                sp.wait_ge(x_in[q], 16)
                sp.sem_inc(x_here, 1)

            def body(j, par, q):
                if has_b(j, -3):
                    jq, jp = (q - 1, 0) if par else (q - 2, 1)
                    wait(sp, ob_done, j - 2)
                    sp.dma_start(out_v[jq, :, jp * 2 * D:(jp + 1) * 2 * D] if isinstance(jq, int)
                                 else out_v[bass.ds(jq, 1), :, jp * 2 * D:(jp + 1) * 2 * D].rearrange("o p d -> (o p) d"),
                                 ob[:, jp].rearrange("p t d -> p (t d)")).then_inc(stored[jp], 16)
            for j in range(-2, 1):
                body(j, j % 2, j // 2)
            iterations_b(sp, body)
            for par in range(2):
                sp.wait_ge(stored[par], 16 * (NP // 2))

        @block.tensor
        def _(pe):
            pe.wait_ge(cT_in, 16)
            pe.wait_ge(wk_in, 16)
            for m in range(KC):
                for k in range(KC):
                    mm = nc.tensor.matmul(bank[:, m // 2, (m % 2) * B * S:(m % 2 + 1) * B * S],
                                          wk_f[:, k, m * P:(m + 1) * P], cT[:, k, :], start=(k == 0), stop=(k == KC - 1))
            mm.then_inc(k_mm, 1)
            pe.wait_ge(wv_in, 16)
            for b in range(B):
                for k in range(KC):
                    mm = nc.tensor.matmul(bank[0:S, 2 + b, :], cT[:, k, b * S:(b + 1) * S], wv_f[:, k, :],
                                          start=(k == 0), stop=(k == KC - 1))
            mm.then_inc(v_mm, 1)
            pe.wait_ge(consts_set, 32)

            def gates():
                pe.wait_ge(fq_in, 16)
                pe.wait_ge(rt_in, 16)
                for m in range(KC):
                    for k in range(KC):
                        mm = nc.tensor.matmul(bank[:, 4 + m // 2, (m % 2) * 256:(m % 2) * 256 + NI],
                                              fq_f[:, k, m * P:(m + 1) * P], rt_f[:, k, :], start=(k == 0), stop=(k == KC - 1))
                mm.then_inc(g_mm, 1)

            def scores(i, g, par, b):
                n = 4 * i + g
                if g % 2 == 0:
                    wait(pe, ql_done, 2 * i + g // 2 + 1)
                wait(pe, sub_done, n - 1)
                for a, w in PASSES:
                    mm = nc.tensor.matmul(s_bank(n2(g)), qT[:, par, a, g, :], kd[:, b, w, g, :],
                                          start=(a == w == 0), stop=(w == 1))
                mm.then_inc(s_mm, 1)

            def n2(g):
                return g % 2

            def probs_T(i, g):
                n = 4 * i + g
                wait(pe, exp_done, n + 1)
                wait(pe, pTh_done, n - 1)
                wait(pe, pTl_done, n - 1)
                for c in range(RC):
                    mm = nc.tensor.transpose(pT_bank(n2(g))[:, c * P:(c + 1) * P], pr[:, n2(g), c * CR:(c + 1) * CR], ident[:])
                mm.then_inc(pT_mm, 1)

            def pv(i, g, b):
                n = 4 * i + g
                wait(pe, pTh_done, n + 1)
                wait(pe, pTl_done, n + 1)
                if g % 2 == 0:
                    wait(pe, cx_done, 2 * i + g // 2 - 1)
                for c in range(RC):
                    at = ((g % 2) * HG + c) * VW
                    for a, w in PASSES:
                        mm = nc.tensor.matmul(
                            o_bank(g // 2)[:, at:at + 2 * VW], pT[0:CR, n2(g), a, c * P:(c + 1) * P],
                            vd[0:CR, c, b, w, g, :, :], start=(g % 2 == 0 and c == 0 and a == w == 0),
                            stop=(g % 2 == 1 and c == RC - 1 and w == 1), skip_group_check=True)
                mm.then_inc(pv_mm, 1)

            def x_T(i, par):
                wait(pe, xnh_done, i + 1)
                wait(pe, xnl_done, i + 1)
                wait(pe, cxT_ready, i - 2)
                for a in range(2):
                    for k in range(KC):
                        at = (a * KC + k) * P
                        mm = nc.tensor.transpose(tr_bank[:, at:at + P], xnh[:, 0, a, k * P:(k + 1) * P], ident16[:])
                mm.then_inc(xT_mm, 1)

            def q_chunks(i, ms):
                if ms[0] == 0:
                    wait(pe, xT_ready, i + 1)
                    wait(pe, x2_done, i - 2)
                for m in ms:
                    for n, (a, w) in enumerate(PASSES):
                        for k in range(KC):
                            at = (a * KC + k) * P
                            mm = nc.tensor.matmul(qw_bank[:, m * P:(m + 1) * P], wq_s[:, w, k, m * P:(m + 1) * P],
                                                  xT[:, 0, at:at + P], start=(n == k == 0), stop=(n == 2 and k == KC - 1))
                if ms[-1] == KC - 1:
                    mm.then_inc(q_mm, 1)

            def ctx_T(i):
                wait(pe, cxh_done, 2 * i + 2)
                wait(pe, cxl_done, 2 * i + 2)
                wait(pe, xT_ready, min(i + 3, NT) if isinstance(i, int) else i + 3)
                for a in range(2):
                    for k in range(KC):
                        at = (a * KC + k) * P
                        mm = nc.tensor.transpose(tr_bank[:, at:at + P], cxh[:, a, k * P:(k + 1) * P], ident16[:])
                mm.then_inc(cxT_mm, 1)

            def project(i, ks):
                if ks[0] == 0:
                    wait(pe, cxT_ready, i + 1)
                    wait(pe, qf_done, min(i + 3, NT) if isinstance(i, int) else i + 3)
                for k in ks:
                    for a, w in PASSES:
                        at = (a * KC + k) * P
                        mm = nc.tensor.matmul(qw_bank, cxT[:, at:at + P], wo_s[:, w, k, :],
                                              start=(k == a == w == 0), stop=(k == KC - 1 and w == 1))
                if ks[-1] == KC - 1:
                    mm.then_inc(wo_mm, 1)

            first = []

            def body(i, par, b, b_before):
                if isinstance(i, int) and i == 0:
                    gates()
                for g in range(NG):
                    if has(i, 0):
                        if isinstance(i, int) and i == 0 and g == 0:
                            pe.wait_ge(hi_set[K_], 1)
                            pe.wait_ge(lo_set[K_], 1)
                            pe.wait_ge(kf_done, 1)
                            pe.wait_ge(vf_done, 1)
                        scores(i, g, par, b)
                    if g == 0 and has(i, -1):
                        probs_T(i - 1, 3)
                    if g > 0 and has(i, 0):
                        probs_T(i, g - 1)
                    if g < 2 and has(i, -1):
                        pv(i - 1, g + 2, b_before)
                    if g >= 2 and has(i, 0):
                        if isinstance(i, int) and i == 0 and g == 2:
                            pe.wait_ge(vd_ones, 1)
                            pe.wait_ge(vd_in, 16 * 6)
                            pe.wait_ge(gf_done, 1)
                        pv(i, g - 2, b)
                    if g == 0:
                        if has(i, -2):
                            project(i - 2, [2, 3])
                        if has(i, 1):
                            x_T(i + 1, 1 - par)
                    if g == 1 and has(i, 1):
                        if not first:
                            first.append(1)
                            pe.wait_ge(hi_set[WQ_], 1)
                            pe.wait_ge(lo_set[WQ_], 1)
                        q_chunks(i + 1, [0, 1])
                    if g == 2:
                        if has(i, 1):
                            q_chunks(i + 1, [2, 3])
                        if has(i, -1):
                            ctx_T(i - 1)
                    if g == 3 and has(i, -1):
                        if isinstance(i, int) and i == 1:
                            pe.wait_ge(hi_set[WO_], 1)
                            pe.wait_ge(lo_set[WO_], 1)
                        project(i - 1, [0, 1])

            def leaf_values():
                pe.wait_ge(wout_in, 16)
                pe.wait_ge(lf_in, 16)
                pe.wait_ge(cxT_ready, NT)
                pe.wait_ge(x2_done, NT)
                for m in range(LC):
                    for k in range(KC):
                        mm = nc.tensor.matmul(bank[:, 6 + m, :], lf_f[:, k, m * P:(m + 1) * P], wout_f[:, k, :],
                                              start=(k == 0), stop=(k == KC - 1))
                mm.then_inc(lv_mm, 1)

            def body_b(j, par, q):
                if has_b(j, -2):
                    if isinstance(j, int) and j == 2:
                        pe.wait_ge(scaled[LV_], 1)
                    wait(pe, lph_done, j - 1)
                    wait(pe, lpl_done, j - 1)
                    wait(pe, lT_ready, j - 2)
                    for t in range(2):
                        for a in range(2):
                            for c in range(LC):
                                at = ((t * 2 + a) * LC + c) * P
                                mm = nc.tensor.transpose(tr_bank[:, at:at + P], lph[:, t, a, c * P:(c + 1) * P], ident16[:])
                    mm.then_inc(lT_mm, 1)
                if has_b(j, 0):
                    if isinstance(j, int) and j == 0:
                        pe.wait_ge(hi_set[G_], 1)
                        pe.wait_ge(lo_set[G_], 1)
                        pe.wait_ge(pTh_done, NG * NT)
                        pe.wait_ge(pTl_done, NG * NT)
                    wait(pe, b_xT_ready, j + 1)
                    wait(pe, th_done, j - 1)
                    for t in range(2):
                        for n, (a, w) in enumerate(PASSES):
                            for k in range(KC):
                                at = (a * KC + k) * P
                                mm = nc.tensor.matmul(bank[:, 2 + par, t * 256:t * 256 + NI], xT[:, t, at:at + P],
                                                      g_s[:, w, k, 0:NI], start=(n == k == 0), stop=(n == 2 and k == KC - 1))
                    mm.then_inc(lg_mm, 1)
                if has_b(j, 1):
                    if isinstance(j, int) and j == -1:
                        pe.wait_ge(sub_done, NG * NT)
                    wait(pe, b_xnh, j + 2)
                    wait(pe, b_xnl, j + 2)
                    wait(pe, b_xT_ready, j + 1)
                    for t in range(2):
                        for a in range(2):
                            for k in range(KC):
                                at = (a * KC + k) * P
                                mm = nc.tensor.transpose(bank[:, t, :].bitcast(F16)[:, at:at + P],
                                                         xnh[:, t, a, k * P:(k + 1) * P], ident16[:])
                    mm.then_inc(b_xT_mm, 1)
                if has_b(j, -2):
                    if isinstance(j, int) and j == 2:
                        pe.wait_ge(hi_set[LV_], 1)
                        pe.wait_ge(lo_set[LV_], 1)
                    wait(pe, lT_ready, j - 1)
                    wait(pe, ob_done, j - 2)
                    for t in range(2):
                        for c in range(LC):
                            for a, w in PASSES:
                                at = ((t * 2 + a) * LC + c) * P
                                mm = nc.tensor.matmul(bank[:, 4 + t, :], lT[:, at:at + P], lv_s[:, w, c, :],
                                                      start=(c == a == w == 0), stop=(c == LC - 1 and w == 1))
                    mm.then_inc(mix_mm, 1)
                if isinstance(j, int) and j == 0:
                    leaf_values()
            iterations_a(pe, body, body_b)
            iterations_b(pe, body_b)

        @block.vector
        def _(dve):
            steps = [0]

            def step(instruction):
                instruction.then_inc(scale_step, 1)
                steps[0] += 1
                dve.wait_ge(scale_step, steps[0])

            def scale_of(c, *, also=None):
                if also is not None:
                    step(nc.vector.tensor_tensor(ar[:, c:c + 1], ar[:, c:c + 1], ar[:, also:also + 1], ALU.max))
                step(nc.vector.tensor_scalar(ar[:, c:c + 1], ar[:, c:c + 1], 1e-30, 1.0 / TARGET, ALU.max, ALU.mult))
                nc.vector.reciprocal(sc[:, c:c + 1], ar[:, c:c + 1]).then_inc(scale_set[c], 1)
                dve.wait_ge(scale_set[c], 1)

            def absmax(c, of, axes=AX_X, rows=P):
                nc.vector.tensor_reduce(am[0:rows, c:c + 1], of, axes, ALU.max, apply_absolute_value=True).then_inc(absmax_done, 1)

            def low_half(c, to, of, high, rows=P):
                dve.wait_ge(hi_set[c], 1)
                return nc.vector.scalar_tensor_tensor(to, of, sc[0:rows, c:c + 1], high, ALU.mult, ALU.subtract)

            step(nc.vector.memset(am[:], 0.0))
            dve.wait_ge(wq_in, 16)
            absmax(WQ_, wq_f[:].rearrange("p c s -> p (c s)"))
            dve.wait_ge(small_in, 16 * 4)
            absmax(6, bq_c[:])
            dve.wait_ge(allmax_done, 2)
            scale_of(WQ_, also=6)
            nc.vector.tensor_scalar(bq_c[:], bq_c[:], sc[:, WQ_:WQ_ + 1], None, ALU.mult).then_inc(bq_scaled, 1)
            dve.wait_ge(kf_done, 1)
            absmax(K_, kf[:].rearrange("p c s -> p (c s)"))
            low_half(WQ_, wq_s[:, 1], wq_f[:], wq_s[:, 0]).then_inc(lo_set[WQ_], 1)
            dve.wait_ge(allmax_done, 3)
            scale_of(K_)
            nc.vector.scalar_tensor_tensor(dq[:, DQ_EXP:DQ_EXP + 1], ar[:, WQ_:WQ_ + 1], DK ** -0.5,
                                           ar[:, K_:K_ + 1], ALU.mult, ALU.mult).then_inc(dq_set, 1)

            def keys_and_values():
                dve.wait_ge(v_mm, 1)
                nc.vector.tensor_tensor(vf[:], bank[0:S, 2:4, :], bv_r.unsqueeze(1).to_broadcast([S, B, D]),
                                        ALU.add).then_inc(vf_done, 1)
                dve.wait_ge(vf_done, 1)
                absmax(V_, vf[:].rearrange("p c s -> p (c s)"), rows=S)
                for r in range(HG):
                    rows = slice(r * DK, (r + 1) * DK)
                    for b in range(B):
                        if r == b == 0:
                            dve.wait_ge(hi_set[K_], 1)
                        last = nc.vector.scalar_tensor_tensor(
                            kd[rows, b, 1, :, r * S:(r + 1) * S], kf[rows, :, b * S:(b + 1) * S], sc[rows, K_:K_ + 1],
                            kd[rows, b, 0, :, r * S:(r + 1) * S], ALU.mult, ALU.subtract)
                last.then_inc(lo_set[K_], 1)
                dve.wait_ge(allmax_done, 4)
                scale_of(V_)
                low_half(V_, vh[:, :, 1, :], vf[:], vh[:, :, 0, :], rows=S).then_inc(lo_set[V_], 1)

            def output_weights():
                dve.wait_ge(wo_in, 16)
                absmax(WO_, wo_f[:].rearrange("p c s -> p (c s)"))
                dve.wait_ge(allmax_done, 5)
                scale_of(WO_)
                nc.vector.scalar_tensor_tensor(dq[:, DQ_OUT:DQ_OUT + 1], ar[:, V_:V_ + 1], 1.0,
                                               ar[:, WO_:WO_ + 1], ALU.mult, ALU.mult).then_inc(dq_set, 1)
                low_half(WO_, wo_s[:, 1], wo_f[:], wo_s[:, 0]).then_inc(lo_set[WO_], 1)

            def gates():
                dve.wait_ge(gf_done, 1)
                absmax(G_, gf, mybir.AxisListType.XY)
                dve.wait_ge(allmax_done, 6)
                scale_of(G_)
                nc.vector.tensor_scalar(dq[:, DQ_TANH:DQ_TANH + 1], ar[:, G_:G_ + 1], 0.5, None, ALU.mult).then_inc(dq_set, 1)
                low_half(G_, g_s[:, 1, :, 0:NI], gf, g_s[:, 0, :, 0:NI]).then_inc(lo_set[G_], 1)

            def stats(i, par):
                wait(dve, x_here, x_quarter(i))
                wait(dve, rstd_done, i)
                nc.vector.bn_stats(st6[:, 0, :], tile_of_x(i)).then_inc(stats_done, 1)

            def aggregate(i):
                if isinstance(i, int):
                    wait(dve, stats_done, i + 1)
                nc.vector.bn_aggr(mv[:, 0, :], st6[:, 0, :]).then_inc(aggr_done, 1)

            def x_quarter(i):
                return i // XQ + 1 if isinstance(i, int) else NQ

            def normalise(i):
                wait(dve, rstd_done, i + 1)
                wait(dve, xnl_done, i)
                nc.vector.tensor_scalar(xn[:, 0, :], tile_of_x(i), mv[:, 0, 0:1], rstd[:, 0:1], ALU.subtract,
                                        ALU.mult).then_inc(xn_done, 1)

            def max_sub(i, g):
                n = 4 * i + g
                sv = s_bank(g % 2).rearrange("p (h s) -> p h s", h=HG)
                wait(dve, s_mm, n + 1)
                nc.vector.tensor_reduce(mx[:, g % 2, :], sv, AX_X, ALU.max).then_inc(max_done, 1)
                wait(dve, max_done, n + 1)
                wait(dve, exp_done, n - 1)
                if g == 0 and has(i, 2):
                    wait(dve, stats_done, i + 3)
                nc.vector.tensor_tensor(df[:, g % 2, :].rearrange("p (h s) -> p h s", h=HG), sv,
                                        mx[:, g % 2, :].unsqueeze(2).to_broadcast([P, HG, S]), ALU.subtract).then_inc(sub_done, 1)

            def probs_low(i, g):
                n = 4 * i + g
                wait(dve, pTh_done, n + 1)
                nc.vector.tensor_tensor(pT[0:CR, g % 2, 1, :], pT_bank(g % 2), pT[0:CR, g % 2, 0, :],
                                        ALU.subtract).then_inc(pTl_done, 1)

            def context(i, half):
                n = 2 * i + half
                o = o_bank(half).rearrange("p (h v) -> p h v", v=VW)
                wait(dve, pv_mm, 2 * n + 2)
                nc.vector.reciprocal(rden[:, half, :], o[:, :, DK]).then_inc(rden_done, 1)
                wait(dve, rden_done, n + 1)
                wait(dve, cxl_done, n - 1)
                nc.vector.tensor_tensor(cx[:, half * (D // 2):(half + 1) * (D // 2)].rearrange("p (h v) -> p h v", v=DK),
                                        o[:, :, 0:DK], rden[:, half, :].unsqueeze(2).to_broadcast([P, H // 2, DK]),
                                        ALU.mult).then_inc(cx_done, 1)

            def q_high(i, par):
                wait(dve, qf_done, i + 1)
                wait(dve, s_mm, 4 * (i - 1))
                nc.vector.tensor_copy(qT[:, par, 0], qf).then_inc(qh_done, 1)

            def residual(i):
                wait(dve, wo_mm, i + 1)
                wait(dve, xb_done, i + 1)
                nc.vector.scalar_tensor_tensor(tile_of_x(i), qw_bank, dq[:, DQ_OUT:DQ_OUT + 1], tile_of_x(i),
                                               ALU.mult, ALU.add).then_inc(x2_done, 1)

            def body(i, par, b, b_before):
                if isinstance(i, int) and i == 0:
                    keys_and_values()
                if isinstance(i, int) and i == 1:
                    output_weights()
                for g in range(NG):
                    if g == 0 and has(i, 2):
                        stats(i + 2, par)
                    if g == 1 and has(i, -2):
                        residual(i - 2)
                    if has(i, 0):
                        max_sub(i, g)
                    if g == 3 and has(i, 1):
                        q_high(i + 1, 1 - par)
                    if g == 0 and has(i, 2):
                        aggregate(i + 2)
                    if g == 0 and has(i, -1):
                        probs_low(i - 1, 3)
                    if g > 0 and has(i, 0):
                        probs_low(i, g - 1)
                    if g == 1 and has(i, -1):
                        context(i - 1, 1)
                    if g == 3 and has(i, 0):
                        context(i, 0)
                    if g == 2 and has(i, 2):
                        normalise(i + 2)
                if isinstance(i, int) and i == 1:
                    gates()

            def leaf_values():
                dve.wait_ge(lv_mm, 1)
                absmax(LV_, bank[:, 6:8, :], mybir.AxisListType.XY)
                dve.wait_ge(allmax_done, 7)
                scale_of(LV_)
                nc.vector.tensor_scalar(wout_f[:, 0:LC, :], bank[:, 6:8, :], 1.0, None, ALU.mult).then_inc(scaled[LV_], 1)
                nc.vector.tensor_scalar(dq[:, DQ_MIX:DQ_MIX + 1], ar[:, LV_:LV_ + 1], 1.0 / ROOT, None,
                                        ALU.mult).then_inc(dq_set, 1)
                low_half(LV_, lv_s[:, 1], wout_f[:, 0:LC, :], lv_s[:, 0]).then_inc(lo_set[LV_], 1)

            def body_b(j, par, q):
                if has_b(j, 2):
                    wait(dve, b_rstd, j + 2)
                    for t in range(2):
                        nc.vector.bn_stats(st6[:, t, :], tile_of_x(2 * j + 4 + t)).then_inc(b_stats, 1)
                if has_b(j, 2):
                    if not has_b(j, -1):
                        dve.wait_ge(b_stats, 2 * j + 6)
                if has_b(j, -1):
                    if has_b(j, 2):
                        wait(dve, b_stats, 2 * j + 6)
                    wait(dve, lph_done, j)
                    nc.vector.tensor_tensor(lph[:, :, 1, :], lp[1], lph[:, :, 0, :], ALU.subtract).then_inc(lpl_done, 1)
                if has_b(j, 2):
                    for t in range(2):
                        nc.vector.bn_aggr(mv[:, t, :], st6[:, t, :]).then_inc(b_aggr, 1)
                if has_b(j, -3):
                    jq, jp = (q - 1, 0) if par else (q - 2, 1)
                    wait(dve, mix_mm, j - 2)
                    wait(dve, b_xb, j - 2)
                    wait(dve, stored[jp], 16 * jq)
                    for t in range(2):
                        last = nc.vector.scalar_tensor_tensor(ob[:, jp, t, :], bank[:, 4 + t, :], dq[:, DQ_MIX:DQ_MIX + 1],
                                                              tile_of_x(2 * j - 6 + t), ALU.mult, ALU.add)
                    last.then_inc(ob_done, 1)
                if has_b(j, 2):
                    wait(dve, b_rstd, j + 3)
                    wait(dve, b_xnl, j + 2)
                    if isinstance(j, int) and j == -2:
                        dve.wait_ge(xnl_done, NT)
                    for t in range(2):
                        nc.vector.tensor_scalar(xn[:, t, :], tile_of_x(2 * j + 4 + t), mv[:, t, 0:1], rstd[:, t:t + 1],
                                                ALU.subtract, ALU.mult).then_inc(b_xn, 1)
                if has_b(j, 0):
                    wait(dve, fr_done, 2 * j + 2)
                    nc.vector.tensor_scalar(lp[0][:, :, 0:2], fr[:, :, :, 0], ROOT, None, ALU.mult).then_inc(lvl_done, 1)
                    for lv in range(1, DEPTH):
                        n = 2 ** lv
                        wait(dve, lvl_done, DEPTH * j + lv)
                        dst, src = lp[lv % 2], lp[1 - lv % 2]
                        nc.vector.tensor_tensor(dst[:, :, 0:2 * n].rearrange("p t (n s) -> p t n s", s=2),
                                                src[:, :, 0:n].unsqueeze(3).to_broadcast([P, 2, n, 2]),
                                                fr[:, :, :, n - 1:2 * n - 1].rearrange("p t s n -> p t n s"),
                                                ALU.mult).then_inc(lvl_done, 1)
                if isinstance(j, int) and j == 0:
                    leaf_values()
            iterations_a(dve, body, body_b)
            iterations_b(dve, body_b)

        @block.scalar
        def _(act):
            act.dma_start(bk_c[:], b_K).then_inc(small_in, 16)
            act.dma_start(bq_c[:], b_Q).then_inc(small_in, 16)
            act.dma_start(ident16[:], eye16).then_inc(consts_set, 16)
            act.dma_start(bv_r, b_V.partition_broadcast(S)).then_inc(small_in, 16)
            act.dma_start(oc[:], ones_cols).then_inc(small_in, 16)
            act.dma_start(bo_r[:], b_O.partition_broadcast(P)).then_inc(late_in, 16)
            act.dma_start(ident[:], eye).then_inc(consts_set, 16)
            act.dma_start(bout_r[:], Wout_b.partition_broadcast(P)).then_inc(late_in, 16)

            def high_half(c, to, of, rows=P):
                act.wait_ge(scale_set[c], 1)
                return nc.scalar.activation(to, of, ACT.Copy, scale=sc[0:rows, c:c + 1])

            act.wait_ge(small_in, 16 * 4)
            act.wait_ge(k_mm, 1)
            for m in range(KC):
                last = nc.scalar.activation(kf[:, m, :], bank[:, m // 2, (m % 2) * B * S:(m % 2 + 1) * B * S],
                                            ACT.Identity, bias=bk_c[:, m:m + 1])
            last.then_inc(kf_done, 1)
            high_half(WQ_, wq_s[:, 0], wq_f[:]).then_inc(hi_set[WQ_], 1)

            def keys():
                act.wait_ge(kd_zero, 1)
                for r in range(HG):
                    rows = slice(r * DK, (r + 1) * DK)
                    for b in range(B):
                        if r == b == 0:
                            act.wait_ge(scale_set[K_], 1)
                        last = nc.scalar.activation(kd[rows, b, 0, :, r * S:(r + 1) * S], kf[rows, :, b * S:(b + 1) * S], ACT.Copy,
                                                    scale=sc[rows, K_:K_ + 1])
                last.then_inc(hi_set[K_], 1)

            def x_high(i):
                wait(act, xn_done, i + 1)
                wait(act, xT_mm, i)
                nc.scalar.activation(xnh[:, 0, 0, :], xn[:, 0, :], ACT.Copy).then_inc(xnh_done, 1)

            def x_T_out(i):
                wait(act, xT_mm, i + 1)
                wait(act, q_mm, i)
                nc.scalar.activation(xT[:, 0, :].bitcast(F32), tr_bank.bitcast(F32), ACT.Copy).then_inc(xT_ready, 1)

            def q_bias(i):
                wait(act, q_mm, i + 1)
                wait(act, ql_done, 2 * i)
                for m in range(KC):
                    last = nc.scalar.activation(qf[:, m, :], qw_bank[:, m * P:(m + 1) * P], ACT.Identity, bias=bq_c[:, m:m + 1])
                last.then_inc(qf_done, 1)

            def exp(i, g):
                n = 4 * i + g
                wait(act, sub_done, n + 1)
                wait(act, pT_mm, n - 1)
                nc.scalar.activation(pr[:, g % 2, 0:GS], df[:, g % 2, :], ACT.Exp, scale=dq[:, DQ_EXP:DQ_EXP + 1]).then_inc(exp_done, 1)

            def probs_high(i, g):
                n = 4 * i + g
                wait(act, pT_mm, n + 1)
                wait(act, pv_mm, n - 1)
                nc.scalar.activation(pT[0:CR, g % 2, 0, :], pT_bank(g % 2), ACT.Copy).then_inc(pTh_done, 1)

            def ctx_high(i, half):
                cols = slice(half * (D // 2), (half + 1) * (D // 2))
                wait(act, cx_done, 2 * i + half + 1)
                wait(act, cxT_mm, i)
                nc.scalar.activation(cxh[:, 0, cols], cx[:, cols], ACT.Copy).then_inc(cxh_done, 1)

            def ctx_T_out(i):
                wait(act, cxT_mm, i + 1)
                wait(act, wo_mm, i)
                nc.scalar.activation(cxT.bitcast(F32), tr_bank.bitcast(F32), ACT.Copy).then_inc(cxT_ready, 1)

            def body(i, par, b, b_before):
                if isinstance(i, int) and i == -1:
                    keys()
                if isinstance(i, int) and i == 0:
                    high_half(V_, vh[:, :, 0, :], vf[:], rows=S).then_inc(hi_set[V_], 1)
                    act.wait_ge(g_mm, 1)
                    nc.scalar.activation(gf, bank[:, 4:6, :].rearrange("p a (m n) -> p (a m) n", m=2)[:, :, 0:NI],
                                         ACT.Copy).then_inc(gf_done, 1)
                if isinstance(i, int) and i == 1:
                    high_half(WO_, wo_s[:, 0], wo_f[:]).then_inc(hi_set[WO_], 1)
                for g in range(NG):
                    if g == 0 and has(i, -1):
                        ctx_high(i - 1, 0)
                    if g == 1 and has(i, 1):
                        x_T_out(i + 1)
                    if g == 2 and has(i, -1):
                        ctx_high(i - 1, 1)
                    if g == 3 and has(i, 1):
                        if isinstance(i, int) and i == -1:
                            act.wait_ge(bq_scaled, 1)
                        q_bias(i + 1)
                    if g == 3 and has(i, -1):
                        ctx_T_out(i - 1)
                    if g == 0 and has(i, -1):
                        probs_high(i - 1, 3)
                    if g > 0 and has(i, 0):
                        probs_high(i, g - 1)
                    if has(i, 0):
                        exp(i, g)
                    if g == 3 and has(i, 2):
                        x_high(i + 2)
                if isinstance(i, int) and i == 1:
                    high_half(G_, g_s[:, 0, :, 0:NI], gf).then_inc(hi_set[G_], 1)

            def body_b(j, par, q):
                if has_b(j, -2):
                    wait(act, lT_mm, j - 1)
                    wait(act, mix_mm, j - 2)
                    nc.scalar.activation(lT.bitcast(F32), bank[:, 6, :], ACT.Copy).then_inc(lT_ready, 1)
                if has_b(j, -1):
                    wait(act, lvl_done, DEPTH * j)
                    wait(act, lT_mm, j - 1)
                    nc.scalar.activation(lph[:, :, 0, :], lp[1], ACT.Copy).then_inc(lph_done, 1)
                if has_b(j, 0):
                    wait(act, lg_mm, j + 1)
                    wait(act, fr_done, 2 * j)
                    nc.scalar.activation(th, bank[:, 2 + par, :].rearrange("p (t n) -> p t n", t=2)[:, :, 0:NI], ACT.Tanh,
                                         scale=dq[:, DQ_TANH:DQ_TANH + 1]).then_inc(th_done, 1)
                    wait(act, th_done, j + 1)
                    wait(act, lvl_done, DEPTH * j)
                    nc.scalar.activation(fr[:, :, 0, :], th, ACT.Copy, bias=0.5, scale=-0.5).then_inc(fr_done, 1)
                    nc.scalar.activation(fr[:, :, 1, :], th, ACT.Copy, bias=0.5, scale=0.5).then_inc(fr_done, 1)
                if has_b(j, 1):
                    wait(act, b_xT_mm, j + 2)
                    wait(act, lg_mm, j + 1)
                    nc.scalar.activation(xT[:].bitcast(F32), bank[:, 0:2, :], ACT.Copy).then_inc(b_xT_ready, 1)
                if has_b(j, 2):
                    wait(act, b_xn, 2 * j + 6)
                    wait(act, b_xT_mm, j + 2)
                    nc.scalar.activation(xnh[:, :, 0, :], xn[:], ACT.Copy).then_inc(b_xnh, 1)
                if isinstance(j, int) and j == 0:
                    act.wait_ge(scaled[LV_], 1)
                    high_half(LV_, lv_s[:, 0], wout_f[:, 0:LC, :]).then_inc(hi_set[LV_], 1)
            iterations_a(act, body, body_b)
            iterations_b(act, body_b)

        @block.gpsimd
        def _(pool):
            nc.gpsimd.memset(kd[:], 0.0).then_inc(kd_zero, 1)
            nc.gpsimd.memset(vd[:], 0.0).then_inc(vd_zero, 1)
            nc.gpsimd.memset(pr[:, :, GS:RC * CR], 0.0).then_inc(vd_zero, 1)
            nc.gpsimd.memset(mhalf[:], -0.5).then_inc(vd_zero, 1)
            nc.gpsimd.memset(eps[:], EPS).then_inc(vd_zero, 1)

            def all_max(col, count):
                pool.wait_ge(absmax_done, count)
                nc.gpsimd.partition_all_reduce(ar[:, col:col + 1], am[:, col:col + 1], P, RMAX).then_inc(allmax_done, 1)

            all_max(WQ_, 1)
            all_max(6, 2)
            all_max(K_, 3)
            pool.wait_ge(small_in, 16 * 4)
            pool.wait_ge(vd_zero, 4)
            for c in range(RC):
                for b in range(B):
                    last = nc.gpsimd.tensor_copy(vd[:, c, b, 0, :, :, DK], oc[:, c, :].unsqueeze(1).to_broadcast([P, NG, 2]))
            last.then_inc(vd_ones, 1)

            def rstd_of(i):
                wait(pool, aggr_done, i + 1)
                nc.gpsimd.tensor_tensor(veps[:, 0:1], mv[:, 0, 1:2], eps[:, 0:1], ALU.add).then_inc(veps_done, 1)
                wait(pool, veps_done, i + 1)
                nc.gpsimd.tensor_tensor(rstd[:, 0:1], veps[:, 0:1], mhalf[:, 0:1], ALU.pow).then_inc(rstd_done, 1)

            def q_low(i, par):
                wait(pool, qh_done, i + 1)
                for h in range(2):
                    ms = slice(h * KC // 2, (h + 1) * KC // 2)
                    nc.gpsimd.tensor_tensor(qT[:, par, 1, ms], qf[:, ms], qT[:, par, 0, ms], ALU.subtract).then_inc(ql_done, 1)

            def x_low(i):
                wait(pool, xnh_done, i + 1)
                nc.gpsimd.tensor_tensor(xnh[:, 0, 1, :], xn[:, 0, :], xnh[:, 0, 0, :], ALU.subtract).then_inc(xnl_done, 1)

            def x_bias(i):
                wait(pool, xn_done, i + 1)
                nc.gpsimd.tensor_tensor(tile_of_x(i), tile_of_x(i), bo_r[:], ALU.add).then_inc(xb_done, 1)

            def ctx_low(i, half):
                cols = slice(half * (D // 2), (half + 1) * (D // 2))
                wait(pool, cxh_done, 2 * i + half + 1)
                nc.gpsimd.tensor_tensor(cxh[:, 1, cols], cx[:, cols], cxh[:, 0, cols], ALU.subtract).then_inc(cxl_done, 1)

            def body(i, par, b, b_before):
                if isinstance(i, int) and i == -2:
                    pool.wait_ge(late_in, 32)
                if isinstance(i, int) and i == 0:
                    all_max(V_, 4)
                if isinstance(i, int) and i == 1:
                    all_max(WO_, 5)
                if has(i, -1):
                    ctx_low(i - 1, 0)
                if has(i, 2):
                    rstd_of(i + 2)
                if has(i, -1):
                    ctx_low(i - 1, 1)
                if has(i, 1):
                    q_low(i + 1, 1 - par)
                if has(i, 2):
                    x_low(i + 2)
                    x_bias(i + 2)
                if isinstance(i, int) and i == 1:
                    all_max(G_, 6)

            def body_b(j, par, q):
                if has_b(j, 2):
                    wait(pool, b_aggr, 2 * j + 6)
                    nc.gpsimd.tensor_tensor(veps[:], mv[:, :, 1], eps[:], ALU.add).then_inc(b_veps, 1)
                    wait(pool, b_veps, j + 3)
                    nc.gpsimd.tensor_tensor(rstd[:], veps[:], mhalf[:], ALU.pow).then_inc(b_rstd, 1)
                    wait(pool, b_xnh, j + 3)
                    nc.gpsimd.tensor_tensor(xnh[:, :, 1, :], xn[:], xnh[:, :, 0, :], ALU.subtract).then_inc(b_xnl, 1)
                    for t in range(2):
                        last = nc.gpsimd.tensor_tensor(tile_of_x(2 * j + 4 + t), tile_of_x(2 * j + 4 + t), bout_r[:], ALU.add)
                    last.then_inc(b_xb, 1)
                if isinstance(j, int) and j == 0:
                    all_max(LV_, 7)
            iterations_a(pool, body, body_b)
            iterations_b(pool, body_b)


def kernel(**inputs):
    import concourse.bacc as bacc
    from concourse.bass_utils import run_bass_kernel_spmd

    a = {k: np.asarray(v) for k, v in inputs.items()}
    p = "L0_xattn_"
    f = "L0_ffn_"
    ones_cols = np.zeros((P, RC, 2), np.float16)
    for row in range(GS):
        c = row // CR
        ones_cols[row - c * CR, c, row // S - c] = 1.0
    arrays = {
        "x": a["x"], "ctxT": a["ctx_1024"].reshape(B * S, D).T,
        "W_Q": a[p + "W_Q"], "b_Q": a[p + "b_Q"].reshape(KC, P).T, "W_K": a[p + "W_K"], "b_K": a[p + "b_K"].reshape(KC, P).T,
        "W_V": a[p + "W_V"], "b_V": a[p + "b_V"], "W_O": a[p + "W_O"], "b_O": a[p + "b_O"],
        "Wq": a[f + "Wq"], "routersT": a[f + "routers"].T, "leafvT": a[f + "leaf_values"].T,
        "WoutT": a[f + "Wout_w"].T, "Wout_b": a[f + "Wout_b"],
        "eye": np.eye(P, dtype=np.float32), "eye16": np.eye(P, dtype=np.float16), "ones_cols": ones_cols,
    }
    arrays = {k: np.ascontiguousarray(v) for k, v in arrays.items()}
    nc = bacc.Bacc("TRN2", target_bir_lowering=False, num_devices=1)
    args = {k: nc.dram_tensor(f"in_{k}", v.shape, mybir.dt.from_np(v.dtype), kind="ExternalInput").ap() for k, v in arrays.items()}
    out = nc.dram_tensor("out_x", (B, L, D), F32, kind="ExternalOutput").ap()
    build(nc, out=out, **args)
    r = run_bass_kernel_spmd(nc, [{f"in_{k}": v for k, v in arrays.items()}], core_ids=[0])
    return r.results[0]["out_x"]
```

```python
from contextlib import ExitStack

import numpy as np

import concourse.bass as bass
from concourse import mybir

F32 = mybir.dt.float32
F16 = mybir.dt.float16
ALU = mybir.AluOpType
ACT = mybir.ActivationFunctionType
AX_X = mybir.AxisListType.X
RMAX = bass.bass_isa.ReduceOp.max

P = 128
B, L, S, D = 2, 2048, 77, 512
H, DK = 16, 32
KC = D // P
NT = B * L // P
TPB = NT // B
XQ = 4
NQ = NT // XQ
HG = P // DK
NG = H // HG
GS = HG * S
RC = 3
CR = -(-GS // RC)
VW = DK + 1
DEPTH = 8
M = 2 ** DEPTH
NI = M - 1
LC = M // P
NP = NT // 2
TARGET = 64.0
ROOT = 2.0 ** 15
EPS = 1e-5
PASSES = [(0, 0), (1, 0), (0, 1)]


def build(nc, x, ctxT, W_Q, b_Q, W_K, b_K, W_V, b_V, W_O, b_O, Wq, routersT, leafvT, WoutT, Wout_b,
          eye, eye16, ones_cols, out):
    ctx = ExitStack()
    with ctx:
        def sb(name, shape, dt=F32):
            return ctx.enter_context(nc.sbuf_tensor(name, shape, dt))

        def sem(name):
            return ctx.enter_context(nc.semaphore(name))

        xs = sb("xs", [P, NT * D])
        ident = sb("ident", [P, P])
        ident16 = sb("ident16", [P, P], F16)
        wq_f = sb("wq_f", [P, KC, D])
        wk_f = sb("wk_f", [P, KC, D])
        wv_f = sb("wv_f", [P, KC, D])
        wo_f = sb("wo_f", [P, KC, D])
        fq_f = sb("fq_f", [P, KC, D])
        wout_f = sb("wout_f", [P, KC, D])
        rt_f = sb("rt_f", [P, KC, NI])
        lf_f = sb("lf_f", [P, KC, M])
        cT = sb("cT", [P, KC, B * S])
        bq_c = sb("bq_c", [P, KC])
        bk_c = sb("bk_c", [P, KC])
        bv_room = sb("bv_room", [P, D])
        bv_r = bv_room[0:S]
        bo_r = sb("bo_r", [P, D])
        bout_r = sb("bout_r", [P, D])
        wq_s = sb("wq_s", [P, 2, KC, D], F16)
        wo_s = sb("wo_s", [P, 2, KC, D], F16)
        g_s = sb("g_s", [P, 2, KC, NI + 1], F16)
        lv_s = sb("lv_s", [P, 2, LC, D], F16)
        kf = sb("kf", [P, KC, B * S])
        kd = sb("kd", [P, B, 2, NG, GS], F16)
        vf = sb("vf", [S, B, D])
        v_room = sb("v_room", [P, B, 2, D], F16)
        vh = v_room[0:S]
        vd = sb("vd", [P, RC, B, 2, NG, 2, VW], F16)
        oc = sb("oc", [P, RC, 2], F16)
        am = sb("am", [P, 8])
        ar = sb("ar", [P, 8])
        sc = sb("sc", [P, 8])
        dq = sb("dq", [P, 8])
        st6 = sb("st6", [P, 2, 6])
        mv = sb("mv", [P, 2, 2])
        veps = sb("veps", [P, 2])
        mhalf = sb("mhalf", [P, 2])
        eps = sb("eps", [P, 2])
        rstd = sb("rstd", [P, 2])
        zero = sb("zero", [P, 2])
        shift = sb("shift", [P, 2, 2])
        xn = sb("xn", [P, 2, D])
        xnh = sb("xnh", [P, 2, 2, D], F16)
        xT = sb("xT", [P, 2, 2 * KC * P], F16)
        qf = cT[:].rearrange("p c s -> p (c s)")[:, 0:D].rearrange("p (c t) -> p c t", c=KC)
        qT = sb("qT", [P, 2, 2, KC, P], F16)
        mx = sb("mx", [P, 2, HG])
        df = sb("df", [P, 2, GS])
        pr = sb("pr", [P, 2, RC * CR])
        pT = sb("pT", [P, 2, 2, RC * P], F16)
        rden = sb("rden", [P, 2, H // 2])
        cx = sb("cx", [P, D])
        cxh = sb("cxh", [P, 2, D], F16)
        cxT = v_room[:, 0].rearrange("p a n -> p (a n)")
        lT = v_room[:, 1].rearrange("p a n -> p (a n)")
        lph = bv_room[:].bitcast(F16).rearrange("p (t a m) -> p t a m", t=2, a=2)
        ob = wk_f[:].rearrange("p (a t) n -> p a t n", a=2)
        wv_room = wv_f[:].rearrange("p c n -> p (c n)")
        lp = [wv_room[:, n * 2 * M:(n + 1) * 2 * M].rearrange("p (t m) -> p t m", t=2) for n in range(2)]
        fr = wv_room[:, 4 * M:4 * M + 4 * NI].rearrange("p (t s n) -> p t s n", t=2, s=2)
        th = kf[:].rearrange("p c s -> p (c s)")[:, 0:2 * NI].rearrange("p (t n) -> p t n", t=2)
        gf = fq_f[:, :, 0:NI]
        bank = ctx.enter_context(nc.psum_tensor("bank", [P, 8, 512], F32))

        def lv_f(m):
            return fq_f[:, 0:2, D // 2:D] if m == 0 else bank[:, 5, :].rearrange("p (a n) -> p a n", a=2)

        def lv_half(h, m):
            return lv_s[:, h, m, :].rearrange("p (a n) -> p a n", a=2)

        def tile_of_x(i):
            return xs[:, bass.ds(i * D, D)]

        small_in, bv_in, cT_in, wq_in, wv_in, wo_in = (sem(n) for n in (
            "small_in", "bv_in", "cT_in", "wq_in", "wv_in", "wo_in"))
        wk_in = [sem(f"wk_in{m}") for m in range(KC)]
        x_first_in = sem("x_first_in")
        fq_in, rt_in, wout_in, lf_in, bo_in, bout_in = (sem(n) for n in (
            "fq_in", "rt_in", "wout_in", "lf_in", "bo_in", "bout_in"))
        x_in = [sem(f"x_in{q}") for q in range(NQ)]
        x_here = sem("x_here")
        consts_set, pool_consts = sem("consts_set"), sem("pool_consts")
        k_mm, v_mm, g_mm, lv_mm = (sem(n) for n in ("k_mm", "v_mm", "g_mm", "lv_mm"))
        kf_done, vf_done = sem("kf_done"), sem("vf_done")
        absmax_done, allmax_done, scale_step = sem("absmax_done"), sem("allmax_done"), sem("scale_step")
        hi_set = [sem(f"hi_set{n}") for n in range(6)]
        lo_set = [sem(f"lo_set{n}") for n in range(6)]
        scale_set = [sem(f"scale_set{n}") for n in range(6)]
        wo_scaled, lv_copied = sem("wo_scaled"), sem("lv_copied")
        bq_scaled, gf_done = sem("bq_scaled"), sem("gf_done")
        vd_zero, vd_ones = sem("vd_zero"), sem("vd_ones")
        vd_in = [sem(f"vd_in{b}") for b in range(B)]
        kd_zero = sem("kd_zero")
        stats_done, aggr_done, veps_done, rstd_done, xn_done, xnh_done, xnl_done, xb_done = (sem(n) for n in (
            "stats_done", "aggr_done", "veps_done", "rstd_done", "xn_done", "xnh_done", "xnl_done", "xb_done"))
        xT_mm, xT_ready, q_mm, qf_done, qh_done, ql_done = (sem(n) for n in (
            "xT_mm", "xT_ready", "q_mm", "qf_done", "qh_done", "ql_done"))
        s_mm, max_done, sub_done, exp_done, pT_mm, pTh_done, pTl_done, pv_mm = (sem(n) for n in (
            "s_mm", "max_done", "sub_done", "exp_done", "pT_mm", "pTh_done", "pTl_done", "pv_mm"))
        rden_done, cx_done, cxh_done, cxl_done, cxT_mm, cxT_ready, wo_mm, x2_done = (sem(n) for n in (
            "rden_done", "cx_done", "cxh_done", "cxl_done", "cxT_mm", "cxT_ready", "wo_mm", "x2_done"))
        b_stats, b_aggr, b_veps, b_rstd, b_shift, b_xn, b_xnh, b_xnl, b_xb = (sem(n) for n in (
            "b_stats", "b_aggr", "b_veps", "b_rstd", "b_shift", "b_xn", "b_xnh", "b_xnl", "b_xb"))
        b_xT_mm, b_xT_ready, lg_mm, th_done, fr_done, lvl_done, lph_done, lpl_done = (sem(n) for n in (
            "b_xT_mm", "b_xT_ready", "lg_mm", "th_done", "fr_done", "lvl_done", "lph_done", "lpl_done"))
        lT_mm, lT_ready, mix_mm, ob_done = (sem(n) for n in ("lT_mm", "lT_ready", "mix_mm", "ob_done"))
        stored = [sem("stored0"), sem("stored1")]

        def wait(eng, s, v):
            if not isinstance(v, int) or v > 0:
                eng.wait_ge(s, v)

        WQ_, K_, V_, WO_, G_, LV_ = range(6)
        DQ_EXP, DQ_OUT, DQ_TANH, DQ_MIX = range(4)

        x_v = x.rearrange("b (q p t) d -> (b q) p (t d)", p=P, t=XQ)
        out_v = out.rearrange("b (q p t) d -> (b q) p (t d)", p=P, t=XQ)

        VD_MOVES = HG + RC - 1

        def chunked(w):
            return w.rearrange("(c p) n -> p c n", p=P)

        def s_bank(n2):
            return bank[:, n2, 0:GS]

        def pT_bank(n2):
            return bank[0:CR, 2 + n2, 0:RC * P]

        def o_bank(half):
            return bank[:, 4 + half, 0:H // 2 * VW]

        tr_bank = bank[:, 6, :].bitcast(F16)
        qw_bank = bank[:, 7, :]

        def iterations_a(eng, body, body_b):
            for i in range(-2, 2):
                body(i, i % 2, 0, 0)
            with eng.Fori(1, TPB // 2) as j:
                for par in range(2):
                    body(2 * j + par, par, 0, 0)
            for par in range(2):
                body(TPB + par, par, 1, par)
            with eng.Fori(TPB // 2 + 1, NT // 2 - 1) as j:
                for par in range(2):
                    body(2 * j + par, par, 1, 1)
            for i in range(NT - 2, NT + 1):
                body(i, i % 2, 1, 1)
            body_b(0, 0, 0)
            body(NT + 1, 1, 1, 1)

        def has(i, *offs):
            return not isinstance(i, int) or all(0 <= i + o < NT for o in offs)

        def iterations_b(eng, body):
            for j in range(1, 6):
                body(j, j % 2, j // 2)
            with eng.Fori(3, NQ - 1) as q:
                for par in range(2):
                    body(2 * q + par, par, q)
            for j in range(NP - 2, NP + 3):
                body(j, j % 2, j // 2)

        def mix_bank(p):
            return 0 if isinstance(p, int) and p == NP - 2 else 4

        def has_b(j, *offs):
            return not isinstance(j, int) or all(0 <= j + o < NP for o in offs)

        block = ctx.enter_context(nc.Block())

        @block.sync
        def _(sp):
            sp.dma_start(cT[:], chunked(ctxT)).then_inc(cT_in, 16)
            for m in range(KC):
                ms = slice(m * P, (m + 1) * P)
                sp.dma_start(wk_f[:, :, ms], chunked(W_K)[:, :, ms]).then_inc(wk_in[m], 16)
            sp.dma_start(wq_f[:], chunked(W_Q)).then_inc(wq_in, 16)
            sp.dma_start(wv_f[:], chunked(W_V)).then_inc(wv_in, 16)
            sp.dma_start(xs[:, 0:2 * D], x_v[0, :, 0:2 * D]).then_inc(x_first_in, 16)
            sp.dma_start(bv_r, b_V.partition_broadcast(S)).then_inc(bv_in, 16)
            sp.dma_start(oc[:], ones_cols).then_inc(bv_in, 16)
            sp.dma_start(ident16[:], eye16).then_inc(consts_set, 16)
            sp.dma_start(ident[:], eye).then_inc(consts_set, 16)
            sp.dma_start(xs[:, 2 * D:XQ * D], x_v[0, :, 2 * D:XQ * D]).then_inc(x_in[0], 16)
            sp.dma_start(wo_f[:], chunked(W_O)).then_inc(wo_in, 16)
            sp.dma_start(bo_r[:], b_O.partition_broadcast(P)).then_inc(bo_in, 16)
            sp.dma_start(fq_f[:], chunked(Wq)).then_inc(fq_in, 16)
            sp.dma_start(rt_f[:], chunked(routersT)).then_inc(rt_in, 16)
            sp.dma_start(xs[:, XQ * D:2 * XQ * D], x_v[1]).then_inc(x_in[1], 16)
            sp.wait_ge(x_in[0], 16)
            sp.sem_inc(x_here, 1)
            sp.dma_start(bout_r[:], Wout_b.partition_broadcast(P)).then_inc(bout_in, 16)
            sp.wait_ge(vd_ones, 1)
            for b in range(B):
                sp.wait_ge(lo_set[V_], b + 1)
                for hh in range(HG):
                    s0 = 0
                    while s0 < S:
                        c, row = divmod(hh * S + s0, CR)
                        n = min(S - s0, CR - row)
                        sp.dma_start(vd[row:row + n, c, b, :, :, hh - c, 0:DK],
                                     vh[s0:s0 + n, b].rearrange("p a (g h v) -> p a g h v", g=NG, h=HG)[:, :, :, hh, :]
                                     ).then_inc(vd_in[b], 16)
                        s0 += n
            for q in range(2, NQ):
                sp.dma_start(xs[:, q * XQ * D:(q + 1) * XQ * D], x_v[q]).then_inc(x_in[q], 16)
            sp.dma_start(wout_f[:], chunked(WoutT)).then_inc(wout_in, 16)
            sp.dma_start(lf_f[:], chunked(leafvT)).then_inc(lf_in, 16)
            for q in range(1, NQ):
                sp.wait_ge(x_in[q], 16)
                sp.sem_inc(x_here, 1)

            def body(j, par, q):
                if has_b(j, -3):
                    jq, jp = (q - 1, 0) if par else (q - 2, 1)
                    if isinstance(j, int) and j == NP + 2:
                        for t in range(2):
                            sp.wait_ge(ob_done, 2 * NP - 1 + t)
                            sp.dma_start(out_v[jq, :, (2 * jp + t) * D:(2 * jp + t + 1) * D], ob[:, jp, t, :]).then_inc(stored[jp], 16)
                        return
                    wait(sp, ob_done, 2 * j - 4)
                    sp.dma_start(out_v[jq, :, jp * 2 * D:(jp + 1) * 2 * D] if isinstance(jq, int)
                                 else out_v[bass.ds(jq, 1), :, jp * 2 * D:(jp + 1) * 2 * D].rearrange("o p d -> (o p) d"),
                                 ob[:, jp].rearrange("p t d -> p (t d)")).then_inc(stored[jp], 16)
            body(0, 0, 0)
            iterations_b(sp, body)
            sp.wait_ge(stored[0], 16 * (NP // 2))
            sp.wait_ge(stored[1], 16 * (NP // 2 + 1))

        @block.tensor
        def _(pe):
            pe.wait_ge(cT_in, 16)
            for m in range(KC):
                pe.wait_ge(wk_in[m], 16)
                for k in range(KC):
                    mm = nc.tensor.matmul(bank[:, m // 2, (m % 2) * B * S:(m % 2 + 1) * B * S],
                                          wk_f[:, k, m * P:(m + 1) * P], cT[:, k, :], start=(k == 0), stop=(k == KC - 1))
            mm.then_inc(k_mm, 1)
            pe.wait_ge(wv_in, 16)
            for b in range(B):
                for k in range(KC):
                    mm = nc.tensor.matmul(bank[0:S, 2 + b, :], cT[:, k, b * S:(b + 1) * S], wv_f[:, k, :],
                                          start=(k == 0), stop=(k == KC - 1))
            mm.then_inc(v_mm, 1)
            pe.wait_ge(consts_set, 32)

            def gates(ms):
                pe.wait_ge(fq_in, 16)
                pe.wait_ge(rt_in, 16)
                for m in ms:
                    for k in range(KC):
                        mm = nc.tensor.matmul(bank[:, 4 + m // 2, (m % 2) * 256:(m % 2) * 256 + NI],
                                              fq_f[:, k, m * P:(m + 1) * P], rt_f[:, k, :], start=(k == 0), stop=(k == KC - 1))
                if ms[-1] == KC - 1:
                    mm.then_inc(g_mm, 1)

            def scores(i, g, par, b):
                n = 4 * i + g
                if g % 2 == 0:
                    wait(pe, ql_done, 2 * i + g // 2 + 1)
                wait(pe, sub_done, n - 1)
                for a, w in PASSES:
                    mm = nc.tensor.matmul(s_bank(n2(g)), qT[:, par, a, g, :], kd[:, b, w, g, :],
                                          start=(a == w == 0), stop=(w == 1))
                mm.then_inc(s_mm, 1)

            def n2(g):
                return g % 2

            def probs_T(i, g):
                n = 4 * i + g
                wait(pe, exp_done, n + 1)
                wait(pe, pTh_done, n - 1)
                wait(pe, pTl_done, n - 1)
                for c in range(RC):
                    mm = nc.tensor.transpose(pT_bank(n2(g))[:, c * P:(c + 1) * P], pr[:, n2(g), c * CR:(c + 1) * CR], ident[:])
                mm.then_inc(pT_mm, 1)

            def pv(i, g, b):
                n = 4 * i + g
                wait(pe, pTh_done, n + 1)
                wait(pe, pTl_done, n + 1)
                if g % 2 == 0:
                    wait(pe, cx_done, 2 * i + g // 2 - 1)
                for c in range(RC):
                    at = ((g % 2) * HG + c) * VW
                    for a, w in PASSES:
                        mm = nc.tensor.matmul(
                            o_bank(g // 2)[:, at:at + 2 * VW], pT[0:CR, n2(g), a, c * P:(c + 1) * P],
                            vd[0:CR, c, b, w, g, :, :], start=(g % 2 == 0 and c == 0 and a == w == 0),
                            stop=(g % 2 == 1 and c == RC - 1 and w == 1), skip_group_check=True)
                mm.then_inc(pv_mm, 1)

            def x_T(i, par):
                wait(pe, xnh_done, i + 1)
                wait(pe, xnl_done, i + 1)
                wait(pe, cxT_ready, i - 2)
                for a in range(2):
                    for k in range(KC):
                        at = (a * KC + k) * P
                        mm = nc.tensor.transpose(tr_bank[:, at:at + P], xnh[:, 0, a, k * P:(k + 1) * P], ident16[:])
                mm.then_inc(xT_mm, 1)

            def q_chunks(i, ms):
                if ms[0] == 0:
                    wait(pe, xT_ready, i + 1)
                    wait(pe, x2_done, i - 2)
                for m in ms:
                    for n, (a, w) in enumerate(PASSES):
                        for k in range(KC):
                            at = (a * KC + k) * P
                            mm = nc.tensor.matmul(qw_bank[:, m * P:(m + 1) * P], wq_s[:, w, k, m * P:(m + 1) * P],
                                                  xT[:, 0, at:at + P], start=(n == k == 0), stop=(n == 2 and k == KC - 1))
                if ms[-1] == KC - 1:
                    mm.then_inc(q_mm, 1)

            def ctx_T(i, half):
                wait(pe, cxl_done, 2 * i + half + 1)
                if half == 0:
                    wait(pe, xT_ready, min(i + 3, NT) if isinstance(i, int) else i + 3)
                for a in range(2):
                    for k in range(half * KC // 2, (half + 1) * KC // 2):
                        at = (a * KC + k) * P
                        mm = nc.tensor.transpose(tr_bank[:, at:at + P], cxh[:, a, k * P:(k + 1) * P], ident16[:])
                if half == 1:
                    mm.then_inc(cxT_mm, 1)

            def project(i, ks):
                if ks[0] == 0:
                    wait(pe, cxT_ready, i + 1)
                    wait(pe, qf_done, min(i + 3, NT) if isinstance(i, int) else i + 3)
                for k in ks:
                    for a, w in PASSES:
                        at = (a * KC + k) * P
                        mm = nc.tensor.matmul(qw_bank, cxT[:, at:at + P], wo_s[:, w, k, :],
                                              start=(k == a == w == 0), stop=(k == KC - 1 and w == 1))
                if ks[-1] == KC - 1:
                    mm.then_inc(wo_mm, 1)

            def body(i, par, b, b_before):
                if isinstance(i, int) and i == 0:
                    gates([0])
                if isinstance(i, int) and i == NT:
                    b_x_T(0)
                    project(i - 2, [2, 3])
                    probs_T(i - 1, 3)
                    pv(i - 1, 2, b_before)
                    b_logits(0, 0, [0])
                    pv(i - 1, 3, b_before)
                    b_logits(0, 0, [1])
                    pe.wait_ge(cx_done, 2 * NT)
                    leaf_values(1, [0, 1])
                    ctx_T(i - 1, 0)
                    ctx_T(i - 1, 1)
                    project(i - 1, [0, 1, 2, 3])
                    b_x_T(1)
                    leaf_values(1, [2, 3])
                    return
                if isinstance(i, int) and i > NT:
                    return
                for g in range(NG):
                    if has(i, 0):
                        if isinstance(i, int) and i == TPB and g == 0:
                            pe.wait_ge(vd_in[1], 16 * VD_MOVES)
                        if isinstance(i, int) and i in (0, TPB) and g == 0:
                            pe.wait_ge(lo_set[K_], HG * (b + 1))
                        if isinstance(i, int) and i == 0 and g == 0:
                            pe.wait_ge(kf_done, 1)
                            pe.wait_ge(vf_done, 1)
                        scores(i, g, par, b)
                    if g == 0 and has(i, -1):
                        probs_T(i - 1, 3)
                    if g > 0 and has(i, 0):
                        probs_T(i, g - 1)
                    if g < 2 and has(i, -1):
                        pv(i - 1, g + 2, b_before)
                    if g >= 2 and has(i, 0):
                        if isinstance(i, int) and i == 0 and g == 2:
                            pe.wait_ge(vd_ones, 1)
                            pe.wait_ge(vd_in[0], 16 * VD_MOVES)
                            pe.wait_ge(gf_done, 1)
                        pv(i, g - 2, b)
                    if g < 2 and isinstance(i, int) and i == 0:
                        gates([[1, 2], [3]][g])
                    if g == 0:
                        if has(i, -2):
                            project(i - 2, [2, 3])
                        if has(i, 1):
                            x_T(i + 1, 1 - par)
                    if g == 1 and has(i, 1):
                        if isinstance(i, int) and i == -1:
                            pe.wait_ge(lo_set[WQ_], KC)
                        q_chunks(i + 1, [0, 1])
                    if g == 2:
                        if has(i, 1):
                            q_chunks(i + 1, [2])
                        if has(i, -1):
                            ctx_T(i - 1, 0)
                        if has(i, 1):
                            q_chunks(i + 1, [3])
                        if has(i, -1):
                            ctx_T(i - 1, 1)
                    if g in (1, 2) and isinstance(i, int) and i == NT - 1:
                        if g == 1:
                            pe.wait_ge(x2_done, NT - 2)
                        leaf_values(0, range(2 * g - 2, 2 * g))
                    if g == 3 and isinstance(i, int) and i == NT - 1:
                        pe.wait_ge(lv_copied, 1)
                    if g == 3 and has(i, -1):
                        if isinstance(i, int) and i == 1:
                            pe.wait_ge(lo_set[WO_], 2)
                        project(i - 1, [0, 1])
                        if isinstance(i, int) and i == 1:
                            pe.wait_ge(lo_set[WO_], KC)

            def leaf_values(m, ks):
                pe.wait_ge(wout_in, 16)
                pe.wait_ge(lf_in, 16)
                for k in ks:
                    mm = nc.tensor.matmul(bank[:, (7, 5)[m], :], lf_f[:, k, m * P:(m + 1) * P], wout_f[:, k, :],
                                          start=(k == 0), stop=(k == KC - 1))
                if k == KC - 1:
                    mm.then_inc(lv_mm, 1)

            def b_x_T(p):
                if isinstance(p, int) and p == 0:
                    pe.wait_ge(sub_done, NG * NT)
                wait(pe, b_xnl, 2 * p + 2)
                wait(pe, b_xT_ready, p)
                for t in range(2):
                    for a in range(2):
                        for k in range(KC):
                            at = (a * KC + k) * P
                            mm = nc.tensor.transpose(bank[:, t, :].bitcast(F16)[:, at:at + P],
                                                     xnh[:, t, a, k * P:(k + 1) * P], ident16[:])
                mm.then_inc(b_xT_mm, 1)

            def b_logits(p, par, ts=(0, 1)):
                if isinstance(p, int) and p == 0:
                    pe.wait_ge(lo_set[G_], KC)
                    pe.wait_ge(pTl_done, NG * NT - 1)
                if isinstance(p, int) and p == 1:
                    pe.wait_ge(pTl_done, NG * NT)
                wait(pe, b_xT_ready, p + 1)
                wait(pe, th_done, p - 1)
                for t in ts:
                    for n, (a, w) in enumerate(PASSES):
                        for k in range(KC):
                            at = (a * KC + k) * P
                            mm = nc.tensor.matmul(bank[:, 2 + par, t * 256:t * 256 + NI], xT[:, t, at:at + P],
                                                  g_s[:, w, k, 0:NI], start=(n == k == 0), stop=(n == 2 and k == KC - 1))
                if t == 1:
                    mm.then_inc(lg_mm, 1)

            def b_leaf_T(p):
                if isinstance(p, int) and p == 0:
                    pe.wait_ge(cxT_ready, NT)
                wait(pe, lpl_done, p + 1)
                wait(pe, lT_ready, p)
                for t in range(2):
                    for a in range(2):
                        for c in range(LC):
                            at = ((t * 2 + a) * LC + c) * P
                            mm = nc.tensor.transpose(tr_bank[:, at:at + P], lph[:, t, a, c * P:(c + 1) * P], ident16[:])
                mm.then_inc(lT_mm, 1)

            def b_mix(p):
                at_bank = mix_bank(p)
                if isinstance(p, int) and p == 0:
                    pe.wait_ge(lo_set[LV_], LC)
                wait(pe, lT_ready, p + 1)
                for t in range(2):
                    if at_bank == 4:
                        wait(pe, ob_done, 2 * p + t - 1)
                    for c in range(LC):
                        for a, w in PASSES:
                            at = ((t * 2 + a) * LC + c) * P
                            mm = nc.tensor.matmul(bank[:, at_bank + t, :], lT[:, at:at + P], lv_s[:, w, c, :],
                                                  start=(c == a == w == 0), stop=(c == LC - 1 and w == 1))
                    mm.then_inc(mix_mm, 1)

            def body_b(j, par, q):
                if isinstance(j, int) and j == 0:
                    return
                if has_b(j, -2):
                    b_leaf_T(j - 2)
                if has_b(j, 0):
                    b_logits(j, par)
                if has_b(j, 1):
                    b_x_T(j + 1)
                if has_b(j, -2):
                    b_mix(j - 2)
            iterations_a(pe, body, body_b)
            iterations_b(pe, body_b)

        @block.vector
        def _(dve):
            steps = [0]

            def step(instruction):
                instruction.then_inc(scale_step, 1)
                steps[0] += 1
                dve.wait_ge(scale_step, steps[0])

            def scale_of(c, *, also=None):
                if also is not None:
                    step(nc.vector.tensor_tensor(ar[:, c:c + 1], ar[:, c:c + 1], ar[:, also:also + 1], ALU.max))
                step(nc.vector.tensor_scalar(ar[:, c:c + 1], ar[:, c:c + 1], 1e-30, 1.0 / TARGET, ALU.max, ALU.mult))
                nc.vector.reciprocal(sc[:, c:c + 1], ar[:, c:c + 1]).then_inc(scale_set[c], 1)
                dve.wait_ge(scale_set[c], 1)

            def absmax(c, of, axes=AX_X, rows=P):
                nc.vector.tensor_reduce(am[0:rows, c:c + 1], of, axes, ALU.max, apply_absolute_value=True).then_inc(absmax_done, 1)

            def low_half(c, to, of, high, rows=P):
                dve.wait_ge(hi_set[c], 1)
                return nc.vector.scalar_tensor_tensor(to, of, sc[0:rows, c:c + 1], high, ALU.mult, ALU.subtract)

            step(nc.vector.memset(am[:], 0.0))
            dve.wait_ge(wq_in, 16)
            absmax(WQ_, wq_f[:].rearrange("p c s -> p (c s)"))
            dve.wait_ge(small_in, 16 * 2)
            absmax(6, bq_c[:])
            dve.wait_ge(allmax_done, 2)
            scale_of(WQ_, also=6)
            nc.vector.tensor_scalar(bq_c[:], bq_c[:], sc[:, WQ_:WQ_ + 1], None, ALU.mult).then_inc(bq_scaled, 1)

            def query_weights_low(ks):
                for k in ks:
                    dve.wait_ge(hi_set[WQ_], k + 1)
                    nc.vector.scalar_tensor_tensor(wq_s[:, 1, k, :], wq_f[:, k, :], sc[:, WQ_:WQ_ + 1], wq_s[:, 0, k, :],
                                                   ALU.mult, ALU.subtract).then_inc(lo_set[WQ_], 1)

            def keys_max():
                dve.wait_ge(kf_done, 1)
                absmax(K_, kf[:].rearrange("p c s -> p (c s)"))

            def keys_scale():
                dve.wait_ge(allmax_done, 3)
                scale_of(K_)
                nc.vector.scalar_tensor_tensor(dq[:, DQ_EXP:DQ_EXP + 1], ar[:, WQ_:WQ_ + 1], DK ** -0.5,
                                               ar[:, K_:K_ + 1], ALU.mult, ALU.mult)

            def keys_low(b):
                for r in range(HG):
                    rows = slice(r * DK, (r + 1) * DK)
                    dve.wait_ge(hi_set[K_], HG * b + r + 1)
                    nc.vector.scalar_tensor_tensor(
                        kd[rows, b, 1, :, r * S:(r + 1) * S], kf[rows, :, b * S:(b + 1) * S], sc[rows, K_:K_ + 1],
                        kd[rows, b, 0, :, r * S:(r + 1) * S], ALU.mult, ALU.subtract).then_inc(lo_set[K_], 1)

            def values():
                dve.wait_ge(bv_in, 16 * 2)
                dve.wait_ge(v_mm, 1)
                nc.vector.tensor_tensor(vf[:], bank[0:S, 2:4, :], bv_r.unsqueeze(1).to_broadcast([S, B, D]),
                                        ALU.add).then_inc(vf_done, 1)
                dve.wait_ge(vf_done, 1)
                absmax(V_, vf[:].rearrange("p c s -> p (c s)"), rows=S)

            def values_scale():
                dve.wait_ge(allmax_done, 4)
                scale_of(V_)

            def values_low(b):
                dve.wait_ge(hi_set[V_], b + 1)
                nc.vector.scalar_tensor_tensor(vh[:, b, 1, :], vf[:, b, :], sc[0:S, V_:V_ + 1], vh[:, b, 0, :],
                                               ALU.mult, ALU.subtract).then_inc(lo_set[V_], 1)

            def output_weights_max(c, half):
                dve.wait_ge(wo_in, 16)
                absmax(c, wo_f[:, 2 * half:2 * half + 2].rearrange("p c s -> p (c s)"))

            def output_weights_scale():
                dve.wait_ge(allmax_done, 6)
                scale_of(WO_, also=7)
                nc.vector.scalar_tensor_tensor(dq[:, DQ_OUT:DQ_OUT + 1], ar[:, V_:V_ + 1], 1.0,
                                               ar[:, WO_:WO_ + 1], ALU.mult, ALU.mult)

            def gates_max(c, half):
                dve.wait_ge(gf_done, 1)
                absmax(c, gf[:, 2 * half:2 * half + 2], mybir.AxisListType.XY)

            def gates_scale():
                dve.wait_ge(allmax_done, 8)
                scale_of(G_, also=7)
                nc.vector.tensor_scalar(dq[:, DQ_TANH:DQ_TANH + 1], ar[:, G_:G_ + 1], 0.5, None, ALU.mult)

            def gates_low(k):
                dve.wait_ge(hi_set[G_], k + 1)
                nc.vector.scalar_tensor_tensor(g_s[:, 1, k, 0:NI], gf[:, k, :], sc[:, G_:G_ + 1], g_s[:, 0, k, 0:NI],
                                               ALU.mult, ALU.subtract).then_inc(lo_set[G_], 1)

            def stats(i):
                if isinstance(i, int) and i < 2:
                    dve.wait_ge(x_first_in, 16)
                else:
                    wait(dve, x_here, x_quarter(i))
                wait(dve, rstd_done, i)
                nc.vector.bn_stats(st6[:, 0, :], tile_of_x(i)).then_inc(stats_done, 1)

            def aggregate(i):
                if isinstance(i, int):
                    wait(dve, stats_done, i + 1)
                nc.vector.bn_aggr(mv[:, 0, :], st6[:, 0, :]).then_inc(aggr_done, 1)

            def x_quarter(i):
                return i // XQ + 1 if isinstance(i, int) else NQ

            def normalise(i):
                wait(dve, rstd_done, i + 1)
                wait(dve, xnl_done, i)
                nc.vector.tensor_scalar(xn[:, 0, :], tile_of_x(i), mv[:, 0, 0:1], rstd[:, 0:1], ALU.subtract,
                                        ALU.mult).then_inc(xn_done, 1)

            def s_of(g):
                return s_bank(g % 2).rearrange("p (h s) -> p h s", h=HG)

            def row_max(i, g):
                wait(dve, s_mm, 4 * i + g + 1)
                nc.vector.tensor_reduce(mx[:, g % 2, :], s_of(g), AX_X, ALU.max).then_inc(max_done, 1)

            def less_max(i, g):
                n = 4 * i + g
                wait(dve, max_done, n + 1)
                wait(dve, exp_done, n - 1)
                if g == 2 and has(i, 2):
                    wait(dve, stats_done, i + 3)
                nc.vector.tensor_tensor(df[:, g % 2, :].rearrange("p (h s) -> p h s", h=HG), s_of(g),
                                        mx[:, g % 2, :].unsqueeze(2).to_broadcast([P, HG, S]), ALU.subtract).then_inc(sub_done, 1)

            def probs_low(i, g):
                n = 4 * i + g
                wait(dve, pTh_done, n + 1)
                nc.vector.tensor_tensor(pT[0:CR, g % 2, 1, :], pT_bank(g % 2), pT[0:CR, g % 2, 0, :],
                                        ALU.subtract).then_inc(pTl_done, 1)

            def ctx_of(half):
                return o_bank(half).rearrange("p (h v) -> p h v", v=VW)

            def inverse_sums(i, half):
                n = 2 * i + half
                wait(dve, pv_mm, 2 * n + 2)
                nc.vector.reciprocal(rden[:, half, :], ctx_of(half)[:, :, DK]).then_inc(rden_done, 1)

            def context(i, half):
                n = 2 * i + half
                wait(dve, rden_done, n + 1)
                wait(dve, cxl_done, n - 1)
                nc.vector.tensor_tensor(cx[:, half * (D // 2):(half + 1) * (D // 2)].rearrange("p (h v) -> p h v", v=DK),
                                        ctx_of(half)[:, :, 0:DK], rden[:, half, :].unsqueeze(2).to_broadcast([P, H // 2, DK]),
                                        ALU.mult).then_inc(cx_done, 1)

            def q_bias(i):
                wait(dve, q_mm, i + 1)
                wait(dve, ql_done, 2 * i)
                nc.vector.tensor_tensor(qf, qw_bank.rearrange("p (c t) -> p c t", c=KC),
                                        bq_c[:].unsqueeze(2).to_broadcast([P, KC, P]), ALU.add).then_inc(qf_done, 1)

            def q_high(i, par, half):
                ms = slice(half * KC // 2, (half + 1) * KC // 2)
                wait(dve, qf_done, i + 1)
                wait(dve, s_mm, 4 * (i - 1))
                nc.vector.tensor_copy(qT[:, par, 0, ms], qf[:, ms]).then_inc(qh_done, 1)

            def residual(i):
                wait(dve, wo_mm, i + 1)
                wait(dve, xb_done, i + 1)
                nc.vector.scalar_tensor_tensor(tile_of_x(i), qw_bank, dq[:, DQ_OUT:DQ_OUT + 1], tile_of_x(i),
                                               ALU.mult, ALU.add).then_inc(x2_done, 1)

            def body(i, par, b, b_before):
                if isinstance(i, int) and i == -2:
                    query_weights_low([0, 1])
                for g in range(NG):
                    if isinstance(i, int) and i == -2 and g == 2:
                        query_weights_low([2])
                    if isinstance(i, int) and i == -2 and g == 3:
                        query_weights_low([3])
                    if isinstance(i, int) and i == -1 and g == 3:
                        values_scale()
                        keys_low(0)
                    if isinstance(i, int) and i == 0 and g == 1:
                        output_weights_max(WO_, 0)
                        output_weights_max(7, 1)
                    if isinstance(i, int) and i == 0 and g == 2:
                        output_weights_scale()
                    if g == 3 and has(i, 1):
                        if isinstance(i, int) and i == -1:
                            dve.wait_ge(bq_scaled, 1)
                        q_bias(i + 1)
                        q_high(i + 1, 1 - par, 0)
                    if isinstance(i, int) and i == -1 and g == 3:
                        normalise(i + 2)
                        values_low(0)
                    if has(i, 0):
                        row_max(i, g)
                    if g == 3 and has(i, 1):
                        q_high(i + 1, 1 - par, 1)
                    if isinstance(i, int) and i == -1 and g == 3:
                        values_low(1)
                    if g < 2 and has(i, -1):
                        inverse_sums(i - 1, g)
                    if has(i, 0):
                        less_max(i, g)
                    if g == 2 and has(i, 2):
                        aggregate(i + 2)
                    if g == 0 and has(i, -1):
                        probs_low(i - 1, 3)
                        context(i - 1, 0)
                    if g == 3 and has(i, 2) and not (isinstance(i, int) and i == -1):
                        normalise(i + 2)
                    if g == 3 and isinstance(i, int) and i == NT - 2:
                        b_normalise(0)
                    if g > 0 and has(i, 0):
                        probs_low(i, g - 1)
                    if g == 0 and has(i, -2) and not (isinstance(i, int) and i > NT):
                        residual(i - 2)
                    if g == 1 and has(i, -1):
                        context(i - 1, 1)
                    if g == 1 and has(i, 2):
                        stats(i + 2)
                    if isinstance(i, int) and i == TPB and g in (1, 2):
                        gates_max((G_, 7)[g - 1], g - 1)
                    if isinstance(i, int) and i == TPB + 1:
                        if g == 0:
                            gates_scale()
                        else:
                            gates_low(g - 1)
                            if g == 3:
                                gates_low(3)
                    if g == 0 and isinstance(i, int) and i == NT - 1:
                        b_normalise(1)
                    if g == 1 and isinstance(i, int) and i in (NT - 2, NT - 1):
                        b_statistics(i - NT + 2)
                    if g == 2 and isinstance(i, int) and i in (NT - 2, NT - 1):
                        b_aggregate(i - NT + 2)
                if isinstance(i, int) and i == -2:
                    keys_max()
                    values()
                    keys_scale()
                if isinstance(i, int) and i == 0:
                    keys_low(1)

            def leaf_values_max():
                dve.wait_ge(lv_copied, 1)
                absmax(LV_, lv_f(0), mybir.AxisListType.XY)
                dve.wait_ge(lv_mm, LC)
                absmax(7, lv_f(1), mybir.AxisListType.XY)

            def leaf_values_split():
                dve.wait_ge(allmax_done, 10)
                scale_of(LV_, also=7)
                nc.vector.tensor_scalar(dq[:, DQ_MIX:DQ_MIX + 1], ar[:, LV_:LV_ + 1], 1.0 / ROOT, None,
                                        ALU.mult)
                for m in range(LC):
                    dve.wait_ge(hi_set[LV_], m + 1)
                    nc.vector.scalar_tensor_tensor(lv_half(1, m), lv_f(m), sc[:, LV_:LV_ + 1], lv_half(0, m),
                                                   ALU.mult, ALU.subtract).then_inc(lo_set[LV_], 1)

            def b_normalise(t):
                dve.wait_ge(b_rstd, 1)
                dve.wait_ge(xnl_done, NT)
                nc.vector.tensor_scalar(xn[:, t, :], tile_of_x(t), mv[:, t, 0:1], rstd[:, t:t + 1], ALU.subtract,
                                        ALU.mult).then_inc(b_xn, 1)

            def b_statistics(p):
                for t in range(2):
                    nc.vector.bn_stats(st6[:, t, :], tile_of_x(2 * p + t)).then_inc(b_stats, 1)

            def b_aggregate(p):
                if isinstance(p, int):
                    dve.wait_ge(b_stats, 2 * p + 2)
                    wait(dve, b_shift, 2 * p)
                for t in range(2):
                    nc.vector.bn_aggr(mv[:, t, :], st6[:, t, :]).then_inc(b_aggr, 1)

            def b_result(p, par, q):
                wait(dve, b_xb, 2 * p + 2)
                wait(dve, stored[par], 16 * q)
                for t in range(2):
                    wait(dve, mix_mm, 2 * p + t + 1)
                    nc.vector.scalar_tensor_tensor(ob[:, par, t, :], bank[:, mix_bank(p) + t, :], dq[:, DQ_MIX:DQ_MIX + 1],
                                                   tile_of_x(2 * p + t), ALU.mult, ALU.add).then_inc(ob_done, 1)

            def b_leaf_low(p, statistics_of):
                if statistics_of is not None:
                    wait(dve, b_stats, 2 * statistics_of + 2)
                    wait(dve, b_shift, 2 * statistics_of)
                wait(dve, lph_done, p + 1)
                nc.vector.tensor_tensor(lph[:, :, 1, :], lp[1], lph[:, :, 0, :], ALU.subtract).then_inc(lpl_done, 1)

            def b_leaves(p):
                wait(dve, fr_done, 2 * p + 2)
                nc.vector.tensor_scalar(lp[0][:, :, 0:2], fr[:, :, :, 0], ROOT, None, ALU.mult).then_inc(lvl_done, 1)
                for lv in range(1, DEPTH):
                    n = 2 ** lv
                    wait(dve, lvl_done, DEPTH * p + lv)
                    dst, src = lp[lv % 2], lp[1 - lv % 2]
                    nc.vector.tensor_tensor(dst[:, :, 0:2 * n].rearrange("p t (n s) -> p t n s", s=2),
                                            src[:, :, 0:n].unsqueeze(3).to_broadcast([P, 2, n, 2]),
                                            fr[:, :, :, n - 1:2 * n - 1].rearrange("p t s n -> p t n s"),
                                            ALU.mult).then_inc(lvl_done, 1)

            def body_b(j, par, q):
                if has_b(j, 2):
                    b_statistics(j + 2)
                jq, jp = (q - 1, 0) if par else (q - 2, 1)
                if has_b(j, -3) and not has_b(j, 2):
                    b_result(j - 3, jp, jq)
                if has_b(j, -1):
                    b_leaf_low(j - 1, j + 2 if has_b(j, 2) else None)
                if has_b(j, 2):
                    b_aggregate(j + 2)
                if has_b(j, -3, 2):
                    b_result(j - 3, jp, jq)
                if isinstance(j, int) and j == 1:
                    leaf_values_max()
                if has_b(j, 0):
                    b_leaves(j)
                if isinstance(j, int) and j == 0:
                    residual(NT - 1)
                if isinstance(j, int) and j == 1:
                    leaf_values_split()
            iterations_a(dve, body, body_b)
            iterations_b(dve, body_b)

        @block.scalar
        def _(act):
            act.dma_start(bk_c[:], b_K).then_inc(small_in, 16)
            act.dma_start(bq_c[:], b_Q).then_inc(small_in, 16)

            def high_half(c, to, of, rows=P):
                act.wait_ge(scale_set[c], 1)
                return nc.scalar.activation(to, of, ACT.Copy, scale=sc[0:rows, c:c + 1])

            act.wait_ge(pool_consts, 2)
            nc.scalar.activation(dq[:, 7:8], mhalf[:, 0:1], ACT.Exp)
            for k in range(KC):
                high_half(WQ_, wq_s[:, 0, k, :], wq_f[:, k, :]).then_inc(hi_set[WQ_], 1)
            act.wait_ge(small_in, 16 * 2)
            act.wait_ge(k_mm, 1)
            for m in range(KC):
                last = nc.scalar.activation(kf[:, m, :], bank[:, m // 2, (m % 2) * B * S:(m % 2 + 1) * B * S],
                                            ACT.Identity, bias=bk_c[:, m:m + 1])
            last.then_inc(kf_done, 1)

            def keys(b):
                act.wait_ge(kd_zero, 1)
                act.wait_ge(scale_set[K_], 1)
                for r in range(HG):
                    rows = slice(r * DK, (r + 1) * DK)
                    nc.scalar.activation(kd[rows, b, 0, :, r * S:(r + 1) * S], kf[rows, :, b * S:(b + 1) * S], ACT.Copy,
                                         scale=sc[rows, K_:K_ + 1]).then_inc(hi_set[K_], 1)

            def x_high(i):
                wait(act, xn_done, i + 1)
                wait(act, xT_mm, i)
                nc.scalar.activation(xnh[:, 0, 0, :], xn[:, 0, :], ACT.Copy).then_inc(xnh_done, 1)

            def x_T_out(i):
                wait(act, xT_mm, i + 1)
                wait(act, q_mm, i)
                nc.scalar.activation(xT[:, 0, :].bitcast(F32), tr_bank.bitcast(F32), ACT.Copy).then_inc(xT_ready, 1)

            def exp(i, g):
                n = 4 * i + g
                wait(act, sub_done, n + 1)
                wait(act, pT_mm, n - 1)
                nc.scalar.activation(pr[:, g % 2, 0:GS], df[:, g % 2, :], ACT.Exp, scale=dq[:, DQ_EXP:DQ_EXP + 1]).then_inc(exp_done, 1)

            def probs_high(i, g):
                n = 4 * i + g
                wait(act, pT_mm, n + 1)
                wait(act, pv_mm, n - 1)
                nc.scalar.activation(pT[0:CR, g % 2, 0, :], pT_bank(g % 2), ACT.Copy).then_inc(pTh_done, 1)

            def ctx_high(i, half):
                cols = slice(half * (D // 2), (half + 1) * (D // 2))
                wait(act, cx_done, 2 * i + half + 1)
                wait(act, cxT_mm, i)
                nc.scalar.activation(cxh[:, 0, cols], cx[:, cols], ACT.Copy).then_inc(cxh_done, 1)

            def ctx_T_out(i):
                wait(act, cxT_mm, i + 1)
                wait(act, wo_mm, i)
                nc.scalar.activation(cxT.bitcast(F32), tr_bank.bitcast(F32), ACT.Copy).then_inc(cxT_ready, 1)

            def output_weights(k):
                high_half(WO_, wo_f[:, k, :], wo_f[:, k, :]).then_inc(wo_scaled, 1)
                act.wait_ge(wo_scaled, k + 1)
                nc.scalar.activation(wo_s[:, 0, k, :], wo_f[:, k, :], ACT.Copy).then_inc(hi_set[WO_], 1)

            def body(i, par, b, b_before):
                for g in range(NG):
                    if isinstance(i, int) and i == -1 and g == 2:
                        keys(0)
                        high_half(V_, vh[:, 0, 0, :], vf[:, 0, :], rows=S).then_inc(hi_set[V_], 1)
                        x_high(i + 2)
                        high_half(V_, vh[:, 1, 0, :], vf[:, 1, :], rows=S).then_inc(hi_set[V_], 1)
                    if isinstance(i, int) and i == 0 and g == 2:
                        act.wait_ge(g_mm, 1)
                        nc.scalar.activation(gf, bank[:, 4:6, :].rearrange("p a (m n) -> p (a m) n", m=2)[:, :, 0:NI],
                                             ACT.Copy).then_inc(gf_done, 1)
                    if g == 1 and has(i, 1):
                        x_T_out(i + 1)
                    if g == 2 and has(i, -1):
                        ctx_high(i - 1, 1)
                    if g == 3 and has(i, -1):
                        ctx_T_out(i - 1)
                    if g == 3 and isinstance(i, int) and i == NT - 1:
                        act.wait_ge(lv_mm, 1)
                        act.wait_ge(hi_set[G_], KC)
                        nc.scalar.activation(lv_f(0), bank[:, 7, :].rearrange("p (a n) -> p a n", a=2), ACT.Copy).then_inc(lv_copied, 1)
                    if isinstance(i, int) and (i, g) == (NT, 0):
                        b_x_T_out(0)
                    if g == 0 and has(i, -1):
                        probs_high(i - 1, 3)
                    if g > 0 and has(i, 0):
                        probs_high(i, g - 1)
                    if has(i, 0):
                        exp(i, g)
                    if g == 0 and has(i, -1):
                        ctx_high(i - 1, 0)
                    if isinstance(i, int) and i == TPB + 1:
                        high_half(G_, g_s[:, 0, g, 0:NI], gf[:, g, :]).then_inc(hi_set[G_], 1)
                    if isinstance(i, int) and (i, g) == (NT - 2, 3):
                        b_x_high(0, 0)
                    if isinstance(i, int) and (i, g) == (NT - 1, 1):
                        b_x_high(0, 1)
                    if isinstance(i, int) and (i, g) == (NT, 2):
                        for t in range(2):
                            b_x_normalise(1, t)
                            b_x_high(1, t)
                    if g == 3 and has(i, 2) and not (isinstance(i, int) and i == -1):
                        x_high(i + 2)
                    if isinstance(i, int) and (i, g) == (0, 0):
                        keys(1)
                    if isinstance(i, int) and (i, g) in ((0, 2), (0, 3), (1, 0), (1, 1)):
                        output_weights(NG * i + g - 2)

            def b_x_normalise(p, t):
                wait(act, b_shift, 2 * p + 2)
                wait(act, b_xnl, 2 * p + t - 1)
                nc.scalar.activation(xn[:, t, :], tile_of_x(2 * p + t), ACT.Identity, bias=shift[:, 1, t:t + 1],
                                     scale=rstd[:, t:t + 1]).then_inc(b_xn, 1)

            def b_x_high(p, t):
                wait(act, b_xn, 2 * p + t + 1)
                wait(act, b_xT_mm, p)
                nc.scalar.activation(xnh[:, t, 0, :], xn[:, t, :], ACT.Copy).then_inc(b_xnh, 1)

            def b_x_T_out(p):
                wait(act, b_xT_mm, p + 1)
                wait(act, lg_mm, p)
                nc.scalar.activation(xT[:].bitcast(F32), bank[:, 0:2, :], ACT.Copy).then_inc(b_xT_ready, 1)

            def b_branches(p, par):
                wait(act, lg_mm, p + 1)
                wait(act, fr_done, 2 * p)
                nc.scalar.activation(th, bank[:, 2 + par, :].rearrange("p (t n) -> p t n", t=2)[:, :, 0:NI], ACT.Tanh,
                                     scale=dq[:, DQ_TANH:DQ_TANH + 1]).then_inc(th_done, 1)
                wait(act, th_done, p + 1)
                wait(act, lvl_done, DEPTH * p)
                nc.scalar.activation(fr[:, :, 0, :], th, ACT.Copy, bias=0.5, scale=-0.5).then_inc(fr_done, 1)
                nc.scalar.activation(fr[:, :, 1, :], th, ACT.Copy, bias=0.5, scale=0.5).then_inc(fr_done, 1)

            def b_leaf_T_out(p):
                wait(act, lT_mm, p + 1)
                wait(act, mix_mm, 2 * p)
                nc.scalar.activation(lT.bitcast(F32), bank[:, 6, :], ACT.Copy).then_inc(lT_ready, 1)

            def b_leaf_high(p):
                wait(act, lvl_done, DEPTH * (p + 1))
                wait(act, lT_mm, p)
                nc.scalar.activation(lph[:, :, 0, :], lp[1], ACT.Copy).then_inc(lph_done, 1)

            def body_b(j, par, q):
                if isinstance(j, int) and j == NP:
                    b_leaf_T_out(j - 2)
                if has_b(j, -1):
                    b_leaf_high(j - 1)
                if has_b(j, -2) and not (isinstance(j, int) and j == NP):
                    b_leaf_T_out(j - 2)
                if has_b(j, 0):
                    b_branches(j, par)
                if has_b(j, 2):
                    b_x_normalise(j + 2, 0)
                if has_b(j, 1):
                    b_x_T_out(j + 1)
                if has_b(j, 2):
                    b_x_high(j + 2, 0)
                    b_x_normalise(j + 2, 1)
                    b_x_high(j + 2, 1)
                if isinstance(j, int) and j == 1:
                    for m in range(LC):
                        high_half(LV_, lv_half(0, m), lv_f(m)).then_inc(hi_set[LV_], 1)
            iterations_a(act, body, body_b)
            iterations_b(act, body_b)

        @block.gpsimd
        def _(pool):
            nc.gpsimd.memset(mhalf[:], -0.5).then_inc(pool_consts, 1)
            nc.gpsimd.memset(eps[:], EPS).then_inc(pool_consts, 1)
            nc.gpsimd.memset(zero[:], 0.0).then_inc(pool_consts, 1)
            nc.gpsimd.memset(kd[:], 0.0).then_inc(kd_zero, 1)
            nc.gpsimd.memset(vd[:], 0.0).then_inc(vd_zero, 1)
            nc.gpsimd.memset(pr[:, :, GS:RC * CR], 0.0).then_inc(vd_zero, 1)

            def all_max(col, count):
                pool.wait_ge(absmax_done, count)
                nc.gpsimd.partition_all_reduce(ar[:, col:col + 1], am[:, col:col + 1], P, RMAX).then_inc(allmax_done, 1)

            all_max(WQ_, 1)
            all_max(6, 2)

            def columns_of_ones():
                pool.wait_ge(bv_in, 16 * 2)
                pool.wait_ge(vd_zero, 2)
                for c in range(RC):
                    for b in range(B):
                        last = nc.gpsimd.tensor_copy(vd[:, c, b, 0, :, :, DK], oc[:, c, :].unsqueeze(1).to_broadcast([P, NG, 2]))
                last.then_inc(vd_ones, 1)

            def output_weights_low(ks):
                for k in ks:
                    pool.wait_ge(hi_set[WO_], k + 1)
                    nc.gpsimd.tensor_tensor(wo_s[:, 1, k, :], wo_f[:, k, :], wo_s[:, 0, k, :],
                                            ALU.subtract).then_inc(lo_set[WO_], 1)

            def rstd_of(i):
                wait(pool, aggr_done, i + 1)
                nc.gpsimd.tensor_tensor(veps[:, 0:1], mv[:, 0, 1:2], eps[:, 0:1], ALU.add).then_inc(veps_done, 1)
                wait(pool, veps_done, i + 1)
                nc.gpsimd.tensor_tensor(rstd[:, 0:1], veps[:, 0:1], mhalf[:, 0:1], ALU.pow).then_inc(rstd_done, 1)

            def q_low(i, par):
                for h in range(2):
                    wait(pool, qh_done, 2 * i + h + 1)
                    ms = slice(h * KC // 2, (h + 1) * KC // 2)
                    nc.gpsimd.tensor_tensor(qT[:, par, 1, ms], qf[:, ms], qT[:, par, 0, ms], ALU.subtract).then_inc(ql_done, 1)

            def x_low(i):
                wait(pool, xnh_done, i + 1)
                nc.gpsimd.tensor_tensor(xnh[:, 0, 1, :], xn[:, 0, :], xnh[:, 0, 0, :], ALU.subtract).then_inc(xnl_done, 1)

            def x_bias(i):
                wait(pool, xn_done, i + 1)
                nc.gpsimd.tensor_tensor(tile_of_x(i), tile_of_x(i), bo_r[:], ALU.add).then_inc(xb_done, 1)

            def ctx_low(i, half):
                cols = slice(half * (D // 2), (half + 1) * (D // 2))
                wait(pool, cxh_done, 2 * i + half + 1)
                nc.gpsimd.tensor_tensor(cxh[:, 1, cols], cx[:, cols], cxh[:, 0, cols], ALU.subtract).then_inc(cxl_done, 1)

            def body(i, par, b, b_before):
                if has(i, -1):
                    ctx_low(i - 1, 0)
                if has(i, -1):
                    ctx_low(i - 1, 1)
                if isinstance(i, int) and i == 1:
                    output_weights_low([2])
                if isinstance(i, int) and i == 0:
                    all_max(WO_, 5)
                    all_max(7, 6)
                if has(i, 2):
                    rstd_of(i + 2)
                if isinstance(i, int) and i == TPB:
                    all_max(G_, 7)
                    all_max(7, 8)
                if isinstance(i, int) and i == 1:
                    output_weights_low([3])
                if isinstance(i, int) and i == NT - 1:
                    b_x_low(0, [1])
                if isinstance(i, int) and i in (NT - 2, NT - 1):
                    b_rstd_of(i - NT + 2)
                if has(i, 1):
                    q_low(i + 1, 1 - par)
                if isinstance(i, int) and i == NT - 2:
                    b_x_low(0, [0])
                if isinstance(i, int) and i == NT - 1:
                    pool.wait_ge(bout_in, 16)
                    b_x_bias(0, 0)
                    b_x_bias(0, 1)
                if isinstance(i, int) and i == NT:
                    b_x_low(1)
                if has(i, 2):
                    x_low(i + 2)
                if isinstance(i, int) and i == -2:
                    all_max(K_, 3)
                    columns_of_ones()
                    all_max(V_, 4)
                if isinstance(i, int) and i == -1:
                    pool.wait_ge(bo_in, 16)
                    x_bias(0)
                if has(i, 2) and not (isinstance(i, int) and i == -2):
                    x_bias(i + 2)
                if isinstance(i, int) and i == 0:
                    output_weights_low([0, 1])

            def b_rstd_of(p):
                wait(pool, b_aggr, 2 * p + 2)
                wait(pool, b_xn, 2 * p)
                nc.gpsimd.tensor_tensor(veps[:], mv[:, :, 1], eps[:], ALU.add).then_inc(b_veps, 1)
                wait(pool, b_veps, p + 1)
                nc.gpsimd.tensor_tensor(rstd[:], veps[:], mhalf[:], ALU.pow).then_inc(b_rstd, 1)
                wait(pool, b_rstd, p + 1)
                nc.gpsimd.tensor_tensor(shift[:, 0, :], mv[:, :, 0], rstd[:], ALU.mult).then_inc(b_shift, 1)
                wait(pool, b_shift, 2 * p + 1)
                nc.gpsimd.tensor_tensor(shift[:, 1, :], zero[:], shift[:, 0, :], ALU.subtract).then_inc(b_shift, 1)

            def b_x_low(p, ts=(0, 1)):
                for t in ts:
                    wait(pool, b_xnh, 2 * p + t + 1)
                    nc.gpsimd.tensor_tensor(xnh[:, t, 1, :], xn[:, t, :], xnh[:, t, 0, :], ALU.subtract).then_inc(b_xnl, 1)

            def b_x_bias(p, t):
                nc.gpsimd.tensor_tensor(tile_of_x(2 * p + t), tile_of_x(2 * p + t), bout_r[:], ALU.add).then_inc(b_xb, 1)

            def body_b(j, par, q):
                if has_b(j, 2):
                    b_rstd_of(j + 2)
                if isinstance(j, int) and j == 1:
                    all_max(LV_, 9)
                    all_max(7, 10)
                if has_b(j, 1):
                    b_x_bias(j + 1, 0)
                    b_x_bias(j + 1, 1)
                if has_b(j, 2):
                    b_x_low(j + 2)
            iterations_a(pool, body, body_b)
            iterations_b(pool, body_b)


def kernel(**inputs):
    import concourse.bacc as bacc
    from concourse.bass_utils import run_bass_kernel_spmd

    a = {k: np.asarray(v) for k, v in inputs.items()}
    p = "L0_xattn_"
    f = "L0_ffn_"
    ones_cols = np.zeros((P, RC, 2), np.float16)
    for row in range(GS):
        c = row // CR
        ones_cols[row - c * CR, c, row // S - c] = 1.0
    arrays = {
        "x": a["x"], "ctxT": a["ctx_1024"].reshape(B * S, D).T,
        "W_Q": a[p + "W_Q"], "b_Q": a[p + "b_Q"].reshape(KC, P).T, "W_K": a[p + "W_K"], "b_K": a[p + "b_K"].reshape(KC, P).T,
        "W_V": a[p + "W_V"], "b_V": a[p + "b_V"], "W_O": a[p + "W_O"], "b_O": a[p + "b_O"],
        "Wq": a[f + "Wq"], "routersT": a[f + "routers"].T, "leafvT": a[f + "leaf_values"].T,
        "WoutT": a[f + "Wout_w"].T, "Wout_b": a[f + "Wout_b"],
        "eye": np.eye(P, dtype=np.float32), "eye16": np.eye(P, dtype=np.float16), "ones_cols": ones_cols,
    }
    arrays = {k: np.ascontiguousarray(v) for k, v in arrays.items()}
    nc = bacc.Bacc("TRN2", target_bir_lowering=False, num_devices=1)
    args = {k: nc.dram_tensor(f"in_{k}", v.shape, mybir.dt.from_np(v.dtype), kind="ExternalInput").ap() for k, v in arrays.items()}
    out = nc.dram_tensor("out_x", (B, L, D), F32, kind="ExternalOutput").ap()
    build(nc, out=out, **args)
    r = run_bass_kernel_spmd(nc, [{f"in_{k}": v for k, v in arrays.items()}], core_ids=[0])
    return r.results[0]["out_x"]
```
